# Optimizing a Trainium2 kernel written in Bass

```python
import numpy as np
import jax
import jax.numpy as jnp

def _softmax(x, axis=-1):
    return jax.nn.softmax(x, axis=axis)

def _gelu(x):
    return jax.nn.gelu(x, approximate=True)

def _silu(x):
    return jax.nn.silu(x)

def _sigmoid(x):
    return jax.nn.sigmoid(x)

def _layernorm(x, axis=-1, eps=1e-05):
    m = jnp.mean(x, axis=axis, keepdims=True)
    v = jnp.var(x, axis=axis, keepdims=True)
    return (x - m) / jnp.sqrt(v + eps)

def _scatter_add(tgt, idx, src, axis=0):
    return tgt.at[idx].add(src)

def _segment_sum(src, seg, n):
    return jax.ops.segment_sum(src, seg, n)
kernel_name = 'mk_adaln_attn_ffn_d1_seqx_r4_269f49'

def setup_inputs(seed: int=0):
    np.random.seed(seed)
    _w = jnp.asarray

    def _rec_inputs():
        import jax
        import jax.numpy as jnp
        _rk = jax.random.key(seed)
        x = -7.109e-05 + 0.9999 * jax.random.normal(jax.random.fold_in(_rk, 1), (32, 64, 1024), jnp.float32)
        _lenS = 64 - jax.random.randint(jax.random.fold_in(_rk, 7), (32,), 0, max(1, 64 // 4) + 1, jnp.int32)
        _lenS2 = 64 - jax.random.randint(jax.random.fold_in(_rk, 8), (32,), 0, max(1, 64 // 4) + 1, jnp.int32)
        itok_B_0_15 = jax.random.randint(jax.random.fold_in(_rk, 11), (32,), 0, 16, jnp.int32)
        itok_B_1_7 = jax.random.randint(jax.random.fold_in(_rk, 12), (32,), 1, 8, jnp.int32)
        return (x, itok_B_0_15, itok_B_1_7)
    x, itok_B_0_15, itok_B_1_7 = _rec_inputs()

    def _L0_cond_setup():
        import jax, jax.numpy as jnp
        import numpy as np
        NUM_CONDITIONS = 16
        IN_CH = 64
        OUT_CH = 64
        B = 64
        T = 1024
        key = jax.random.key(seed)
        k_x, k_w, k_c = jax.random.split(key, 3)
        x = jax.random.normal(k_x, (B, IN_CH, T), dtype=jnp.float32)
        bound = float(np.sqrt(6.0 / IN_CH))
        weights = jax.random.uniform(k_w, (NUM_CONDITIONS, IN_CH, OUT_CH), dtype=jnp.float32, minval=-bound, maxval=bound)
        condition = jax.random.randint(k_c, (B,), 0, NUM_CONDITIONS, dtype=jnp.int64)
        return {'x': x, 'weights': weights, 'condition': condition}
    _L0_cond_all = _L0_cond_setup()
    _L0_cond_in = {k: v for k, v in _L0_cond_all.items() if k in ('weights',)}
    del _L0_cond_all

    def _L0_attn_setup():
        import jax, jax.numpy as jnp
        import numpy as np
        import math
        B, S, DM = (1, 512, 1024)
        H, HKV, HD = (32, 8, 128)
        EPS = 1e-06
        NEG_INF = -1e+30

        def _alibi_slopes(n_heads: int) -> np.ndarray:
            start = 2 ** (-2 ** (-(math.log2(n_heads) - 3)))
            return np.array([start * start ** i for i in range(n_heads)], dtype=np.float32)

        def _rmsnorm(t, w):
            tf = t.astype(jnp.float32)
            inv = jax.lax.rsqrt(jnp.mean(tf * tf, axis=-1, keepdims=True) + EPS)
            return (tf * inv * w).astype(t.dtype)
        key = jax.random.key(seed)
        ks = jax.random.split(key, 5)
        std = 0.02
        return {'x': jax.random.normal(ks[0], (B, S, DM), dtype=jnp.float32), 'Wq': jax.random.normal(ks[1], (H * HD, DM), dtype=jnp.float32) * std, 'Wk': jax.random.normal(ks[2], (HKV * HD, DM), dtype=jnp.float32) * std, 'Wv': jax.random.normal(ks[3], (HKV * HD, DM), dtype=jnp.float32) * std, 'Wo': jax.random.normal(ks[4], (H * HD, DM), dtype=jnp.float32).T * (std / math.sqrt(2 * 32)), 'q_norm_w': jnp.ones((HD,), dtype=jnp.float32), 'k_norm_w': jnp.ones((HD,), dtype=jnp.float32)}
    _L0_attn_all = _L0_attn_setup()
    _L0_attn_in = {k: v for k, v in _L0_attn_all.items() if k in ('Wq', 'Wk', 'Wv', 'Wo', 'q_norm_w', 'k_norm_w')}
    del _L0_attn_all

    def _L0_cond2_setup():
        import jax, jax.numpy as jnp
        import numpy as np
        B, S, D_IN, D_OUT = (4, 512, 1024, 1024)
        N_ADAPTERS, MAX_RANK = (8, 16)
        key = jax.random.key(seed)
        ks = jax.random.split(key, 7)
        x = jax.random.normal(ks[0], (B, S, D_IN), dtype=jnp.float32)
        weight = jax.random.normal(ks[1], (D_OUT, D_IN), dtype=jnp.float32) * (1.0 / np.sqrt(D_IN))
        bias = jax.random.normal(ks[2], (D_OUT,), dtype=jnp.float32) * 0.01
        lora_a_weights = jax.random.normal(ks[3], (N_ADAPTERS, MAX_RANK, D_IN), dtype=jnp.float32) * (1.0 / np.sqrt(D_IN))
        lora_b_weights = jax.random.normal(ks[4], (N_ADAPTERS, D_OUT, MAX_RANK), dtype=jnp.float32) * 0.02
        scaling_factors = jax.random.uniform(ks[5], (N_ADAPTERS,), dtype=jnp.float32, minval=0.5, maxval=2.0)
        adapter_id = jax.random.randint(ks[6], (B,), 0, N_ADAPTERS, dtype=jnp.int64)
        return {'x': x, 'weight': weight, 'bias': bias, 'lora_a_weights': lora_a_weights, 'lora_b_weights': lora_b_weights, 'scaling_factors': scaling_factors, 'adapter_id': adapter_id}
    _L0_cond2_all = _L0_cond2_setup()
    _L0_cond2_in = {k: v for k, v in _L0_cond2_all.items() if k in ('weight', 'bias', 'lora_a_weights', 'lora_b_weights', 'scaling_factors')}
    del _L0_cond2_all

    def _L0_ffn_setup():
        import math
        import jax, jax.numpy as jnp
        import numpy as np
        SCALING = 16.0 / 32.0

        def real_fourier_orthogonal_multiply(c):
            n = c.shape[-1]
            sqrt_n = math.sqrt(n)
            pair_scale = math.sqrt(n / 2.0)
            max_f = (n - 1) // 2
            work = c.astype(jnp.float32)
            dc = (work[..., 0] * sqrt_n)[..., None].astype(jnp.complex64)
            cos = work[..., 1:1 + 2 * max_f:2] * pair_scale
            sin = work[..., 2:2 + 2 * max_f:2] * pair_scale
            mid = (cos - 1j * sin).astype(jnp.complex64)
            parts = [dc, mid]
            if n % 2 == 0:
                parts.append((work[..., -1] * sqrt_n)[..., None].astype(jnp.complex64))
            spectrum = jnp.concatenate(parts, axis=-1)
            return jnp.fft.irfft(spectrum, n=n, axis=-1).astype(c.dtype)
        key = jax.random.key(seed)
        ks = jax.random.split(key, 9)
        B, S, D_in, D_out, R0, R1, E = (4, 512, 1024, 1024, 32, 8, 3)
        x = jax.random.normal(ks[0], (B, S, D_in), dtype=jnp.float32)
        W_base = jax.random.normal(ks[1], (D_out, D_in), dtype=jnp.float32) * 0.02
        b_base = jax.random.normal(ks[2], (D_out,), dtype=jnp.float32) * 0.02
        enc0 = jax.random.normal(ks[3], (R0, D_in), dtype=jnp.float32) * 0.02
        enc1 = jax.random.normal(ks[4], (R1, D_in), dtype=jnp.float32) * 0.02
        coefs0 = jax.random.normal(ks[5], (E, D_out, R0), dtype=jnp.float32) * 0.02
        coefs1 = jax.random.normal(ks[6], (E, D_out, R1), dtype=jnp.float32) * 0.02
        mask0 = jax.random.randint(ks[7], (E, D_out, R0), 0, 2).astype(bool)
        mask1 = jax.random.randint(ks[8], (E, D_out, R1), 0, 2).astype(bool)
        return dict(x=x, W_base=W_base, b_base=b_base, enc0=enc0, enc1=enc1, coefs0=coefs0, coefs1=coefs1, mask0=mask0, mask1=mask1)
    _L0_ffn_all = _L0_ffn_setup()
    _L0_ffn_in = {k: v for k, v in _L0_ffn_all.items() if k in ('W_base', 'b_base', 'enc0', 'enc1', 'coefs0', 'coefs1', 'mask0', 'mask1')}
    del _L0_ffn_all
    return {'x': x, 'itok_B_0_15': itok_B_0_15, 'itok_B_1_7': itok_B_1_7, 'L0_cond_weights': _L0_cond_in['weights'], 'L0_attn_Wq': _L0_attn_in['Wq'], 'L0_attn_Wk': _L0_attn_in['Wk'], 'L0_attn_Wv': _L0_attn_in['Wv'], 'L0_attn_Wo': _L0_attn_in['Wo'], 'L0_attn_q_norm_w': _L0_attn_in['q_norm_w'], 'L0_attn_k_norm_w': _L0_attn_in['k_norm_w'], 'L0_cond2_weight': _L0_cond2_in['weight'], 'L0_cond2_bias': _L0_cond2_in['bias'], 'L0_cond2_lora_a_weights': _L0_cond2_in['lora_a_weights'], 'L0_cond2_lora_b_weights': _L0_cond2_in['lora_b_weights'], 'L0_cond2_scaling_factors': _L0_cond2_in['scaling_factors'], 'L0_ffn_W_base': _L0_ffn_in['W_base'], 'L0_ffn_b_base': _L0_ffn_in['b_base'], 'L0_ffn_enc0': _L0_ffn_in['enc0'], 'L0_ffn_enc1': _L0_ffn_in['enc1'], 'L0_ffn_coefs0': _L0_ffn_in['coefs0'], 'L0_ffn_coefs1': _L0_ffn_in['coefs1'], 'L0_ffn_mask0': _L0_ffn_in['mask0'], 'L0_ffn_mask1': _L0_ffn_in['mask1']}

def reference(x, itok_B_0_15, itok_B_1_7, L0_cond_weights, L0_attn_Wq, L0_attn_Wk, L0_attn_Wv, L0_attn_Wo, L0_attn_q_norm_w, L0_attn_k_norm_w, L0_cond2_weight, L0_cond2_bias, L0_cond2_lora_a_weights, L0_cond2_lora_b_weights, L0_cond2_scaling_factors, L0_ffn_W_base, L0_ffn_b_base, L0_ffn_enc0, L0_ffn_enc1, L0_ffn_coefs0, L0_ffn_coefs1, L0_ffn_mask0, L0_ffn_mask1):
    import jax
    import jax.numpy as jnp

    def _L0_cond_ref(x, weights, condition):
        import jax, jax.numpy as jnp
        import numpy as np
        NUM_CONDITIONS = 16
        IN_CH = 64
        OUT_CH = 64
        B = 64
        T = 1024
        W = weights[condition]
        return jnp.einsum('bct,bcd->bdt', x, W)

    def _L0_attn_ref(x, Wq, Wk, Wv, Wo, q_norm_w, k_norm_w):
        import jax, jax.numpy as jnp
        import numpy as np
        import math
        B, S, DM = (1, 512, 1024)
        H, HKV, HD = (32, 8, 128)
        EPS = 1e-06
        NEG_INF = -1e+30

        def _alibi_slopes(n_heads: int) -> np.ndarray:
            start = 2 ** (-2 ** (-(math.log2(n_heads) - 3)))
            return np.array([start * start ** i for i in range(n_heads)], dtype=np.float32)

        def _rmsnorm(t, w):
            tf = t.astype(jnp.float32)
            inv = jax.lax.rsqrt(jnp.mean(tf * tf, axis=-1, keepdims=True) + EPS)
            return (tf * inv * w).astype(t.dtype)
        b, s, _ = x.shape
        G = H // HKV
        q = (x @ Wq.T).reshape(b, s, H, HD).transpose(0, 2, 1, 3)
        k = (x @ Wk.T).reshape(b, s, HKV, HD).transpose(0, 2, 1, 3)
        v = (x @ Wv.T).reshape(b, s, HKV, HD).transpose(0, 2, 1, 3)
        q = _rmsnorm(q, q_norm_w)
        k = _rmsnorm(k, k_norm_w)
        qg = q.reshape(b, HKV, G, s, HD)
        scores = jnp.einsum('bkgqd,bksd->bkgqs', qg, k) / math.sqrt(HD)
        slopes = jnp.asarray(_alibi_slopes(H)).reshape(HKV, G)
        pos = jnp.arange(s, dtype=jnp.float32)
        rel = pos[None, :] - pos[:, None]
        bias = jnp.where(rel > 0, NEG_INF, slopes[:, :, None, None] * rel)
        attn = jax.nn.softmax(scores + bias[None], axis=-1)
        out = jnp.einsum('bkgqs,bksd->bkgqd', attn, v)
        out = out.reshape(b, H, s, HD).transpose(0, 2, 1, 3).reshape(b, s, H * HD)
        return out @ Wo.T

    def _L0_cond2_ref(x, weight, bias, lora_a_weights, lora_b_weights, scaling_factors, adapter_id):
        import jax, jax.numpy as jnp
        import numpy as np
        B, S, D_IN, D_OUT = (4, 512, 1024, 1024)
        N_ADAPTERS, MAX_RANK = (8, 16)
        base = jnp.einsum('bsi,oi->bso', x, weight) + bias
        a_sel = lora_a_weights[adapter_id]
        b_sel = lora_b_weights[adapter_id]
        scale = scaling_factors[adapter_id]
        low = jnp.einsum('bsi,bri->bsr', x, a_sel)
        delta = jnp.einsum('bsr,bor->bso', low, b_sel)
        return base + scale[:, None, None] * delta

    def _L0_ffn_ref(x, W_base, b_base, enc0, enc1, coefs0, coefs1, mask0, mask1):
        import math
        import jax, jax.numpy as jnp
        import numpy as np
        SCALING = 16.0 / 32.0

        def real_fourier_orthogonal_multiply(c):
            n = c.shape[-1]
            sqrt_n = math.sqrt(n)
            pair_scale = math.sqrt(n / 2.0)
            max_f = (n - 1) // 2
            work = c.astype(jnp.float32)
            dc = (work[..., 0] * sqrt_n)[..., None].astype(jnp.complex64)
            cos = work[..., 1:1 + 2 * max_f:2] * pair_scale
            sin = work[..., 2:2 + 2 * max_f:2] * pair_scale
            mid = (cos - 1j * sin).astype(jnp.complex64)
            parts = [dc, mid]
            if n % 2 == 0:
                parts.append((work[..., -1] * sqrt_n)[..., None].astype(jnp.complex64))
            spectrum = jnp.concatenate(parts, axis=-1)
            return jnp.fft.irfft(spectrum, n=n, axis=-1).astype(c.dtype)
        base = jnp.einsum('bsd,od->bso', x, W_base) + b_base
        e0 = jnp.einsum('bsd,rd->bsr', x, enc0)
        e1 = jnp.einsum('bsd,rd->bsr', x, enc1)
        w0 = coefs0 * mask0.astype(coefs0.dtype)
        w1 = coefs1 * mask1.astype(coefs1.dtype)
        decoded = jnp.einsum('bsr,eor->ebso', e0, w0) + jnp.einsum('bsr,eor->ebso', e1, w1)
        transformed = real_fourier_orthogonal_multiply(decoded)
        update = transformed.sum(axis=0)
        return base + update * SCALING
    x = x + _L0_attn_ref(_L0_cond_ref(x, L0_cond_weights, itok_B_0_15), L0_attn_Wq, L0_attn_Wk, L0_attn_Wv, L0_attn_Wo, L0_attn_q_norm_w, L0_attn_k_norm_w)
    x = x + _L0_ffn_ref(_L0_cond2_ref(x, L0_cond2_weight, L0_cond2_bias, L0_cond2_lora_a_weights, L0_cond2_lora_b_weights, L0_cond2_scaling_factors, itok_B_1_7), L0_ffn_W_base, L0_ffn_b_base, L0_ffn_enc0, L0_ffn_enc1, L0_ffn_coefs0, L0_ffn_coefs1, L0_ffn_mask0, L0_ffn_mask1)
    return x

_drawn_inputs = setup_inputs


def setup_inputs(seed=0):
    import zlib

    import numpy as np

    out = dict(_drawn_inputs(seed))
    spreads = {'L0_attn_q_norm_w': (1.0, 0.6), 'L0_attn_k_norm_w': (1.0, 0.6)}
    factors = {'L0_cond2_bias': 8.0,
     'L0_cond2_scaling_factors': 2.895,
     'L0_ffn_b_base': 3.555,
     'L0_ffn_enc1': 2.692,
     'L0_ffn_coefs1': 2.682}
    for name, (base, spread) in spreads.items():
        noise = np.random.default_rng([zlib.crc32(name.encode()), seed]).standard_normal(out[name].shape)
        drawn = base * np.exp(spread * noise) if base else spread * noise
        out[name] = jnp.asarray(drawn.astype(out[name].dtype))
    for name, factor in factors.items():
        out[name] = (out[name] * factor).astype(out[name].dtype)
    return out
```

```python
from contextlib import ExitStack
import math

import numpy as np
import concourse.bass as bass
from concourse import mybir

F32 = mybir.dt.float32
F32R = mybir.dt.float32r
I32 = mybir.dt.int32
U8 = mybir.dt.uint8
ALU = mybir.AluOpType
ACT = mybir.ActivationFunctionType
AXIS = mybir.AxisListType

P = 128
BATCH, SEQ, DM = 32, 64, 1024
KT = DM // P
HEADS, KV_HEADS, HD = 32, 8, 128
GROUP = HEADS // KV_HEADS
TOKENS = BATCH * SEQ
BLOCK = 512
TILES = BLOCK // P
BLOCKS = TOKENS // BLOCK
BPT = P // SEQ
WIDE = 512
UNIT_CHUNKS = 4
CHUNK = 1024
ADAPTERS, RANK = 8, 16
EXPERTS, ENC = 3, 40
EPS = 1e-6
SCALING = 16.0 / 32.0
QUARTERS = 4


class Signal:

    def __init__(self, handle):
        self.handle, self.count = handle, 0


class Queue:

    def __init__(self):
        self.items = []

    def do(self, waits, build, signal=None, by=1):
        if signal is not None:
            signal.count += by
        self.items.append((list(waits), build, signal, by))
        return None if signal is None else (signal, signal.count)

    def emit(self, eng):
        reached = {}
        for waits, build, signal, by in self.items:
            for mark in waits:
                if mark is not None and reached.get(mark[0], 0) < mark[1]:
                    eng.wait_ge(mark[0].handle, mark[1])
                    reached[mark[0]] = mark[1]
            last = build(eng)
            if signal is not None:
                last.then_inc(signal.handle, by)


def build_program(nc, d, out):
    ctx = ExitStack()
    with ctx:
        def sb(name, shape, dt=F32):
            return ctx.enter_context(nc.sbuf_tensor(name, shape, dt))

        def sig(name):
            return Signal(ctx.enter_context(nc.semaphore(name)))

        ring_hi = sb("ring_hi", [P, 2, UNIT_CHUNKS, CHUNK], F32R)
        ring_lo = sb("ring_lo", [P, 2, UNIT_CHUNKS, CHUNK], F32R)
        act_hi = sb("act_hi", [P, KT, BLOCK], F32R)
        act_lo = sb("act_lo", [P, KT, BLOCK], F32R)
        acc = sb("acc", [P, TILES, DM])
        raw = [sb(f"raw{i}", [P, CHUNK]) for i in range(2)]
        kt_hi = sb("kt_hi", [P, 2, BLOCK], F32R)
        kt_lo = sb("kt_lo", [P, 2, BLOCK], F32R)
        v_hi = sb("v_hi", [P, TILES, 2, HD], F32R)
        v_lo = sb("v_lo", [P, TILES, 2, HD], F32R)
        ot_hi = sb("ot_hi", [P, TILES, GROUP, BPT, SEQ], F32R)
        ot_lo = sb("ot_lo", [P, TILES, GROUP, BPT, SEQ], F32R)
        qn = [sb(f"qn{i}", [P, GROUP * HD]) for i in range(2)]
        sq = sb("sq", [P, GROUP * HD])
        qt_hi = sb("qt_hi", [P, BPT, GROUP, SEQ], F32R)
        qt_lo = sb("qt_lo", [P, BPT, GROUP, SEQ], F32R)
        score = sb("score", [P, 256])
        prob = sb("prob", [P, 256])
        pt_hi = sb("pt_hi", [P, 256], F32R)
        pt_lo = sb("pt_lo", [P, 256], F32R)
        alibi = sb("alibi", [P, HEADS // 2, SEQ])
        beff_hi = sb("beff_hi", [P, DM], F32R)
        beff_lo = sb("beff_lo", [P, DM], F32R)
        bias_eff = sb("bias_eff", [P, DM])
        loraa_hi = sb("loraa_hi", [P, KT, P], F32R)
        loraa_lo = sb("loraa_lo", [P, KT, P], F32R)
        mixw_raw = sb("mixw_raw", [P, TILES, P])
        mixw_hi = sb("mixw_hi", [P, TILES, P], F32R)
        mixw_lo = sb("mixw_lo", [P, TILES, P], F32R)
        ident = sb("ident", [P, P])
        kgain = sb("kgain", [P, HD])
        qgain = sb("qgain", [P, HD])
        mixidx = sb("mixidx", [1, BATCH], I32)
        adidx = sb("adidx", [P, BATCH], I32)
        adidf = sb("adidf", [P, BATCH])
        admask = sb("admask", [P, BATCH])
        adrow = sb("adrow", [P, 1])
        adscale = sb("adscale", [P, 1])
        mask8 = sb("mask8", [P, EXPERTS * KT * ENC], U8)
        half = sb("half", [P, GROUP])
        ssum = sb("ssum", [P, GROUP])
        mean = sb("mean", [P, GROUP])
        rstd = sb("rstd", [P, GROUP])
        peak = sb("peak", [P, 4])
        total = sb("total", [P, 4])
        inv = sb("inv", [P, 4])

        main_bank = [ctx.enter_context(nc.psum_tensor(f"main{i}", [P, WIDE], F32)) for i in range(3)]
        qt_bank = ctx.enter_context(nc.psum_tensor("qt_bank", [P, WIDE], F32))
        s_bank = ctx.enter_context(nc.psum_tensor("s_bank", [P, WIDE], F32))
        pt_bank = ctx.enter_context(nc.psum_tensor("pt_bank", [P, WIDE], F32))
        pv_bank = ctx.enter_context(nc.psum_tensor("pv_bank", [P, BPT, WIDE], F32))
        main_free = [None] * 3
        free = {"qt": None, "s": None, "pt": None, "pv": None}

        f_scratch = nc.dram_tensor("f_scratch", [2, UNIT_CHUNKS, P, 2, WIDE], F32).ap()

        PE, AC, VE, PO, SP = Queue(), Queue(), Queue(), Queue(), Queue()

        s_const = sig("s_const")
        s_raw = [sig(f"s_raw{i}") for i in range(2)]
        s_hi, s_lo = sig("s_hi"), sig("s_lo")
        s_fold = sig("s_fold")
        s_main = sig("s_main")
        s_prep = sig("s_prep")
        s_mset = sig("s_mset")
        s_wc = sig("s_wc")
        s_mixhi, s_mixlo = sig("s_mixhi"), sig("s_mixlo")
        s_x = [sig(f"s_x{t}") for t in range(TILES)]
        s_xhi, s_xlo = sig("s_xhi"), sig("s_xlo")
        s_tr = sig("s_tr")
        s_acthi, s_actlo = sig("s_acthi"), sig("s_actlo")
        s_sq, s_sum, s_mean, s_rstd, s_qn = (sig(n) for n in ("s_sq", "s_sum", "s_mean", "s_rstd", "s_qn"))
        s_vhi, s_vlo = sig("s_vhi"), sig("s_vlo")
        s_kthi, s_ktlo = sig("s_kthi"), sig("s_ktlo")
        s_qthi, s_qtlo = sig("s_qthi"), sig("s_qtlo")
        s_sc, s_soft, s_exp, s_prob = sig("s_sc"), sig("s_soft"), sig("s_exp"), sig("s_prob")
        s_pt, s_pthi, s_ptlo = sig("s_pt"), sig("s_pthi"), sig("s_ptlo")
        s_pv, s_othi, s_otlo = sig("s_pv"), sig("s_othi"), sig("s_otlo")
        s_acc = sig("s_acc")
        s_bias = sig("s_bias")
        s_low, s_lowm, s_lowhi, s_lowlo = (sig(n) for n in ("s_low", "s_lowm", "s_lowhi", "s_lowlo"))
        s_evac = sig("s_evac")
        s_fst = [sig(f"s_fst{i}") for i in range(4)]
        s_out = [sig(f"s_out{t}") for t in range(TILES)]
        s_idx = sig("s_idx")

        def f32(ap):
            return ap.bitcast(F32)

        def split(src, hi, lo, waits_hi, waits_lo, sig_hi, sig_lo):
            hi_done = AC.do(waits_hi, lambda e: e.activation(hi, src, ACT.Copy), sig_hi)
            lo_done = VE.do([hi_done, *waits_lo],
                            lambda e: e.tensor_tensor(lo, src, f32(hi), ALU.subtract), sig_lo)
            return hi_done, lo_done

        def products(eng, bank, terms, start, stop):
            last = None
            for n, (lh, ll, rh, rl) in enumerate(terms):
                for m, (a, b) in enumerate(((lh, rh), (lh, rl), (ll, rh))):
                    last = eng.matmul(bank, a, b, start=start and n == 0 and m == 0,
                                      stop=stop and n == len(terms) - 1 and m == 2)
            return last

        consts = 0

        def load_const(dst, src):
            nonlocal consts
            consts += 1
            return AC.do([], lambda e: e.dma_start(dst, src), s_const, 16)

        COEF = EXPERTS * KT * ENC
        coef_raw, coef_masked = acc[:, 0, 0:COEF], acc[:, 1, 0:COEF]
        load_const(coef_raw, d["coefs"])
        load_const(mask8[:, :], d["masks"])
        load_const(ident[:, :], d["identity"])
        load_const(alibi[:, :, :], d["alibi"])
        load_const(bias_eff[:, :], d["b_base"])
        load_const(kgain[:, :], d["k_norm_w"])
        load_const(qgain[:, :], d["q_norm_w"])
        load_const(adidx[:, :], d["adapter_of_batch"])
        load_const(adrow[:, :], d["adapter_of_row"])
        load_const(adscale[:, :], d["adapter_scale"])
        const = (s_const, 16 * consts)
        idx_here = SP.do([], lambda e: e.dma_start(mixidx[:, :], d["mix_of_batch"]), s_idx, 16)
        mset = PO.do([], lambda e: e.memset(mixw_raw[:, :, :], 0.0), s_mset)
        mset = PO.do([], lambda e: e.memset(half[:, :], -0.5), s_mset)

        raw_free = [None, None]
        n_raw = 0
        slot_free = [[None] * UNIT_CHUNKS for _ in range(2)]
        n_unit = 0

        def load_raw(src, rows=P, after=()):
            nonlocal n_raw
            i = n_raw % 2
            n_raw += 1
            here = SP.do([raw_free[i], *after], lambda e: e.dma_start(raw[i][0:rows, :], src), s_raw[i], 16)
            return i, here

        class Unit:

            def __init__(self, chunks, after=()):
                nonlocal n_unit
                self.slot = n_unit % 2
                n_unit += 1
                self.chunks, self.after = chunks, after
                self.marks = [[] for _ in range(UNIT_CHUNKS)]

            def hi(self, c):
                return ring_hi[:, self.slot, c, :]

            def lo(self, c):
                return ring_lo[:, self.slot, c, :]

            def prepare(self, c):
                i, here = load_raw(self.chunks[c], after=self.after)
                f = slot_free[self.slot][c]
                marks = split(raw[i][:, :], self.hi(c), self.lo(c), [here, f], [f], s_hi, s_lo)
                raw_free[i] = marks[1]
                self.marks[c] = marks

            def wide(self, kt):
                a = (kt % 2) * WIDE
                return self.hi(kt // 2)[:, a:a + WIDE], self.lo(kt // 2)[:, a:a + WIDE]

        W40 = KT * ENC
        mark = VE.do([const], lambda e: e.tensor_tensor(coef_masked, coef_raw, mask8[:, :], ALU.mult), s_prep)
        part = [acc[:, 1, e * W40:(e + 1) * W40] for e in range(EXPERTS)]
        mark = VE.do([mark], lambda e: e.tensor_tensor(coef_raw[:, 0:W40], part[0], part[1], ALU.add), s_prep)
        mark = VE.do([mark], lambda e: e.tensor_tensor(coef_raw[:, W40:2 * W40], coef_raw[:, 0:W40], part[2],
                                                       ALU.add), s_prep)
        mark = VE.do([mark], lambda e: e.tensor_scalar(coef_raw[:, 0:W40], coef_raw[:, W40:2 * W40], SCALING, None,
                                                       ALU.mult), s_prep)
        coef_hi = kt_hi[:, :, :].rearrange("p a n -> p (a n)")[:, 0:W40]
        coef_lo = kt_lo[:, :, :].rearrange("p a n -> p (a n)")[:, 0:W40]
        coef_marks = split(coef_raw[:, 0:W40], coef_hi, coef_lo, [mark], [], s_hi, s_lo)
        mark = VE.do([const], lambda e: e.tensor_copy(adidf[:, :], adidx[:, :]), s_prep)
        VE.do([mark], lambda e: e.tensor_scalar(admask[:, :], adidf[:, :], adrow[:, 0:1], adscale[:, 0:1],
                                                ALU.is_equal, ALU.mult), s_prep)
        mark = VE.do([], lambda e: e.tensor_tensor(kgain[:, :], kgain[:, :], qgain[:, :], ALU.mult), s_prep)
        gains = VE.do([mark], lambda e: e.tensor_scalar(kgain[:, :], kgain[:, :], 1.0 / math.sqrt(HD), None,
                                                        ALU.mult), s_prep)

        enc_hi = v_hi[0:ENC, :, :, :].rearrange("p a b n -> p (a b n)")
        enc_lo = v_lo[0:ENC, :, :, :].rearrange("p a b n -> p (a b n)")
        i, here = load_raw(d["encoders"], rows=ENC)
        enc_marks = split(raw[i][0:ENC, :], enc_hi, enc_lo, [here], [], s_hi, s_lo)
        raw_free[i] = enc_marks[1]

        n_main = 0

        def next_bank():
            nonlocal n_main
            b = n_main % 3
            n_main += 1
            return b

        wt_hi = ot_hi[0:ENC, :, :, :, :].rearrange("p a b c n -> p (a b c n)")[:, 0:DM]
        wt_lo = ot_lo[0:ENC, :, :, :, :].rearrange("p a b c n -> p (a b c n)")[:, 0:DM]
        wt_marks = []
        for u in range(2):
            unit = Unit([d["basis"][u, c] for c in range(UNIT_CHUNKS)])
            b = next_bank()
            for c in range(UNIT_CHUNKS):
                unit.prepare(c)
                terms = [(coef_hi[:, kt * ENC:(kt + 1) * ENC], coef_lo[:, kt * ENC:(kt + 1) * ENC], *unit.wide(kt))
                         for kt in (2 * c, 2 * c + 1)]
                done = PE.do([main_free[b], *coef_marks, *unit.marks[c]],
                             lambda e, b=b, c=c, terms=terms: products(e, main_bank[b][0:ENC, :], terms, c == 0,
                                                                       c == UNIT_CHUNKS - 1), s_main)
                slot_free[unit.slot][c] = done
            cols = slice(u * WIDE, (u + 1) * WIDE)
            marks = split(main_bank[b][0:ENC, :], wt_hi[:, cols], wt_lo[:, cols], [done], [], s_hi, s_lo)
            main_free[b] = marks[1]
            wt_marks.append(marks)

        weff = []
        for u in range(2):
            unit = Unit(None)
            weff.append(unit)
            cols = slice(u * WIDE, (u + 1) * WIDE)
            for c in range(UNIT_CHUNKS):
                i, here = load_raw(d["w_base"][u, c])
                for j in range(2):
                    kt = 2 * c + j
                    b = next_bank()
                    rows = slice(kt * P, (kt + 1) * P)
                    term = (enc_hi[:, rows], enc_lo[:, rows], wt_hi[:, cols], wt_lo[:, cols])
                    done = PE.do([main_free[b], *enc_marks, *wt_marks[u]],
                                 lambda e, b=b, term=term: products(e, main_bank[b][:, :], [term], True, True), s_main)
                    part_ap = raw[i][:, j * WIDE:(j + 1) * WIDE]
                    folded = VE.do([here, done], lambda e, b=b, part_ap=part_ap: e.tensor_tensor(
                        part_ap, main_bank[b][:, :], part_ap, ALU.add), s_fold)
                    main_free[b] = folded
                f = slot_free[unit.slot][c]
                unit.marks[c] = split(raw[i][:, :], unit.hi(c), unit.lo(c), [folded, f], [f], s_hi, s_lo)
                raw_free[i] = unit.marks[c][1]

        part_free = [None] * TILES
        f_done = [None] * 4
        n_store = 0
        act_read = []
        for s in range(KT + 2):
            q = s % TILES
            i, here = load_raw(d["w2_units"][s])
            cols = slice(q * P, (q + 1) * P)
            marks = split(raw[i][:, :].rearrange("p (k n) -> p k n", k=KT), act_hi[:, :, cols], act_lo[:, :, cols],
                          [here, part_free[q]], [part_free[q]], s_hi, s_lo)
            raw_free[i] = marks[1]
            for u in range(2):
                b = next_bank()
                for c in range(UNIT_CHUNKS):
                    terms = [(act_hi[:, kt, cols], act_lo[:, kt, cols], *weff[u].wide(kt))
                             for kt in (2 * c, 2 * c + 1)]
                    done = PE.do([main_free[b], *marks, *weff[u].marks[c]],
                                 lambda e, b=b, c=c, terms=terms: products(e, main_bank[b][:, :], terms, c == 0,
                                                                           c == UNIT_CHUNKS - 1), s_main)
                    if s == KT + 1:
                        slot_free[weff[u].slot][c] = done
                oc = slice(u * WIDE, (u + 1) * WIDE)
                if s < KT:
                    st = n_store % 4
                    n_store += 1
                    stage = acc[:, 2 + st // 2, (st % 2) * WIDE:(st % 2 + 1) * WIDE]
                    here = AC.do([done, f_done[st]], lambda e, b=b, stage=stage: e.activation(
                        stage, main_bank[b][:, :], ACT.Copy), s_evac)
                    main_free[b] = here
                    f_done[st] = PO.do([here], lambda e, u=u, s=s, stage=stage: e.dma_start(
                        f_scratch[u, s // 2, :, s % 2, :], stage), s_fst[st], 16)
                elif s == KT:
                    beff_marks = split(main_bank[b][:, :], beff_hi[:, oc], beff_lo[:, oc], [done], [], s_hi, s_lo)
                    main_free[b] = beff_marks[1]
                else:
                    main_free[b] = VE.do([done, const], lambda e, b=b, oc=oc: e.tensor_tensor(
                        bias_eff[:, oc], main_bank[b][:, :], bias_eff[:, oc], ALU.add), s_bias)
                    bias_done = main_free[b]
            part_free[q] = done
        i, here = load_raw(d["lora_a"])
        loraa_marks = split(raw[i][:, :].rearrange("p (k n) -> p k n", k=KT), loraa_hi[:, :, :], loraa_lo[:, :, :],
                            [here], [], s_hi, s_lo)
        raw_free[i] = loraa_marks[1]
        setup_read = done

        main_steps = []
        side = {}
        quarter = [0]

        def later(delay, work):
            side.setdefault(quarter[0] + delay, []).append(work)

        def tick():
            quarter[0] += 1
            for work in side.pop(quarter[0], []):
                work()

        schedule = []
        for blk in range(BLOCKS):
            for g in range(KV_HEADS):
                if g % 2 == 0:
                    schedule.append(("kv", blk, g // 2))
                schedule += [("q", blk, g), ("o", blk, g)]
            schedule += [("f", blk, 0), ("f", blk, 1)]
        sources = {"kv": d["wkv"], "q": d["wq"], "o": d["wo"],
                   "f": f_scratch.rearrange("u c p j n -> u c p (j n)")}
        units = {}
        n_prepared = 0
        acc_free = [list(f_done) for _ in range(TILES)]
        qt_free = [None]

        def prepare_next():
            nonlocal n_prepared
            u, c = divmod(n_prepared, UNIT_CHUNKS)
            if u >= len(schedule):
                return
            kind, blk, n = schedule[u]
            if c == 0:
                if kind == "kv" and n == 0:
                    gather_mix(blk)
                units[u] = Unit([sources[kind][n, j] for j in range(UNIT_CHUNKS)],
                                after=f_done if kind == "f" else ())
            units[u].prepare(c)
            n_prepared += 1

        mix_free = [setup_read]
        mix_state = {}

        def gather_mix(blk):
            for j in range(TILES * BPT):
                t, b = j // BPT, j % BPT
                dst = mixw_raw[b * SEQ:(b + 1) * SEQ, t, b * SEQ:(b + 1) * SEQ]

                def gather(e, batch=blk * TILES * BPT + j, dst=dst):
                    which = e.value_load(mixidx[0:1, batch:batch + 1], min_val=0, max_val=15)
                    return e.dma_start(dst, d["mix_w"][bass.ds(which, 1), :, :].rearrange("a c n -> (a c) n"))
                here = SP.do([idx_here, mset, mix_state.get("split")], gather, s_wc, 16)
            mix_state["here"] = here

        def load_x(blk, t):
            return PO.do(acc_free[t], lambda e: e.dma_start(acc[:, t, :], d["x"][blk * TILES + t]), s_x[t], 16)

        x_here = [load_x(0, t) for t in range(TILES)]
        act_marks = [None] * TILES
        act_free = [setup_read] * TILES
        ot_free = [setup_read] * TILES
        kt_free, v_free = setup_read, setup_read

        def spread_pair(hi, lo, src_banks, dst, waits, frees):
            pass

        def mix(blk, t):
            nonlocal x_here
            if t == 0:
                m = split(mixw_raw[:, :, :], mixw_hi[:, :, :], mixw_lo[:, :, :], [mix_state["here"], mix_free[0]],
                          [mix_free[0]], s_mixhi, s_mixlo)
                mix_state["split"] = m[1]
                mix_state["marks"] = m
            r = t % 2
            xh = ot_hi[:, 2 * r:2 * r + 2, :, :, :].rearrange("p a h b n -> p (a h b n)")
            xl = ot_lo[:, 2 * r:2 * r + 2, :, :, :].rearrange("p a h b n -> p (a h b n)")
            marks = split(acc[:, t, :], xh, xl, [x_here[t], ot_free[2 * r], ot_free[2 * r + 1]], [],
                          s_xhi, s_xlo)
            for half_no, (name, bank) in enumerate((("qt", qt_bank), ("s", s_bank))):
                def run(e, half_no=half_no, bank=bank):
                    for k in range(4):
                        kt = 4 * half_no + k
                        term = (xh[:, kt * P:(kt + 1) * P], xl[:, kt * P:(kt + 1) * P],
                                mixw_hi[:, t, :], mixw_lo[:, t, :])
                        last = products(e, bank[:, k * P:(k + 1) * P], [term], True, True)
                    return last
                done = PE.do([free[name], *marks, *mix_state["marks"]], run, s_tr)
                evacuate_act(t, half_no, name, bank, done)
            mix_free[0] = done
            ot_free[2 * r] = ot_free[2 * r + 1] = done

        def evacuate_act(t, half_no, name, bank, done):
            dst_h = act_hi[:, 4 * half_no:4 * half_no + 4, t * P:(t + 1) * P]
            dst_l = act_lo[:, 4 * half_no:4 * half_no + 4, t * P:(t + 1) * P]
            src = bank[:, :].rearrange("p (k n) -> p k n", k=4)
            marks = split(src, dst_h, dst_l, [done, act_free[t]], [], s_acthi, s_actlo)
            free[name] = marks[1]
            act_marks[t] = marks

        n_norm = 0
        rstd_read = [None]

        def rms_norm(bank, b, heads, done, extra):
            nonlocal n_norm
            dst = qn[n_norm % 2]
            w = heads * HD
            wait_q = qn_free[n_norm % 2]
            n_norm += 1
            squared = AC.do([done, sum_state["sum"]], lambda e: e.activation(sq[:, 0:w], bank[:, 0:w], ACT.Square),
                            s_sq)
            summed = VE.do([squared, sum_state["mean"]], lambda e: e.tensor_reduce(
                ssum[:, 0:heads], sq[:, 0:w].rearrange("p (h n) -> p h n", h=heads), AXIS.X, ALU.add), s_sum)
            sum_state["sum"] = summed
            averaged = VE.do([summed, sum_state["rstd"]], lambda e: e.tensor_scalar(
                mean[:, 0:heads], ssum[:, 0:heads], 1.0 / HD, EPS, ALU.mult, ALU.add), s_mean)
            sum_state["mean"] = averaged
            powered = PO.do([averaged, mset, sum_state["qn"]], lambda e: e.tensor_tensor(
                rstd[:, 0:heads], mean[:, 0:heads], half[:, 0:heads], ALU.pow), s_rstd)
            sum_state["rstd"] = powered
            scaled = VE.do([powered, squared, wait_q, *extra], lambda e: e.tensor_tensor(
                dst[:, 0:w].rearrange("p (h n) -> p h n", h=heads),
                bank[:, 0:w].rearrange("p (h n) -> p h n", h=heads),
                rstd[:, 0:heads].rearrange("p (h o) -> p h o", o=1).broadcast_to([P, heads, HD]), ALU.mult), s_qn)
            sum_state["qn"] = scaled
            main_free[b] = scaled
            return dst, scaled

        sum_state = {"sum": None, "mean": None, "rstd": None, "qn": None}
        qn_free = [None, None]

        def key_transpose(src, ready, slot, t):
            def run(e):
                for j in range(2):
                    last = e.transpose(qt_bank[:, j * P:(j + 1) * P], src[:, j * P:(j + 1) * P], ident[:, :])
                return last
            done = PE.do([ready, free["qt"], const], run, s_tr)
            qn_free[slot] = done
            cols = slice(t * P, (t + 1) * P)
            marks = split(qt_bank[:, 0:2 * P].rearrange("p (j n) -> p j n", j=2), kt_hi[:, :, cols],
                          kt_lo[:, :, cols], [done, kt_free], [kt_free], s_kthi, s_ktlo)
            free["qt"] = marks[1]
            kt_marks[t] = marks

        kt_marks = [None] * TILES
        v_marks = [None] * TILES
        ot_marks = [None] * TILES

        def attend(blk, g, t, src, ready, slot):
            j = g % 2
            state = {}

            def transpose_q():
                def run(e):
                    for h in range(GROUP):
                        last = e.transpose(qt_bank[:, h * P:(h + 1) * P], src[:, h * P:(h + 1) * P], ident[:, :])
                    return last
                done = PE.do([ready, free["qt"], const], run, s_tr)
                qn_free[slot] = done
                bank = qt_bank[:, :].rearrange("p (h b n) -> p h b n", h=GROUP, b=BPT)
                state["qt"] = split(bank, qt_hi[:, :, :, :].rearrange("p b h n -> p h b n"),
                                    qt_lo[:, :, :, :].rearrange("p b h n -> p h b n"),
                                    [done, qt_free[0]], [], s_qthi, s_qtlo)
                free["qt"] = state["qt"][1]

            def scores():
                def run(e):
                    for hp in range(2):
                        for b in range(BPT):
                            a = (hp * BPT + b) * SEQ
                            keys = slice(t * P + b * SEQ, t * P + (b + 1) * SEQ)
                            lh = qt_hi[:, b, 2 * hp:2 * hp + 2, :].rearrange("p h n -> p (h n)")
                            ll = qt_lo[:, b, 2 * hp:2 * hp + 2, :].rearrange("p h n -> p (h n)")
                            last = products(e, s_bank[:, a:a + SEQ], [(lh, ll, kt_hi[:, j, keys], kt_lo[:, j, keys])],
                                            True, True)
                    return last
                done = PE.do([*state["qt"], *kt_marks[t], free["s"]], run, s_sc)
                qt_free[0] = done
                nonlocal kt_read
                kt_read = done
                bank = s_bank[:, 0:256].rearrange("p (h b n) -> p h b n", h=2, b=BPT)
                table = alibi[:, 2 * g:2 * g + 2, :].rearrange("p h (o n) -> p h o n", o=1)\
                    .broadcast_to([P, 2, BPT, SEQ])
                rows = score[:, :].rearrange("p (h b n) -> p h b n", h=2, b=BPT)
                biased = VE.do([done, const, soft["score"]], lambda e: e.tensor_tensor(rows, bank, table, ALU.add),
                               s_soft)
                free["s"] = biased
                by_row = score[:, :].rearrange("p (r n) -> p r n", n=SEQ)
                peaked = VE.do([biased], lambda e: e.tensor_reduce(peak[:, :], by_row, AXIS.X, ALU.max), s_soft)
                shifted = VE.do([peaked], lambda e: e.tensor_tensor(
                    by_row, by_row, peak[:, :].rearrange("p (r o) -> p r o", o=1).broadcast_to([P, 4, SEQ]),
                    ALU.subtract), s_soft)
                powered = AC.do([shifted, soft["prob"]], lambda e: e.activation(prob[:, :], score[:, :], ACT.Exp),
                                s_exp)
                soft["score"] = powered
                state["exp"] = powered

            def normalise():
                p_row = prob[:, :].rearrange("p (r n) -> p r n", n=SEQ)
                summed = VE.do([state["exp"]], lambda e: e.tensor_reduce(total[:, :], p_row, AXIS.X, ALU.add), s_soft)
                inverse = VE.do([summed], lambda e: e.reciprocal(inv[:, :], total[:, :]), s_soft)
                state["prob"] = VE.do([inverse], lambda e: e.tensor_tensor(
                    p_row, p_row, inv[:, :].rearrange("p (r o) -> p r o", o=1).broadcast_to([P, 4, SEQ]),
                    ALU.mult), s_prob)

            def transpose_p():
                def run(e):
                    for hp in range(2):
                        last = e.transpose(pt_bank[:, hp * P:(hp + 1) * P], prob[:, hp * P:(hp + 1) * P], ident[:, :])
                    return last
                done = PE.do([state["prob"], free["pt"], const], run, s_pt)
                soft["prob"] = done
                state["pt"] = split(pt_bank[:, 0:256], pt_hi[:, :], pt_lo[:, :], [done, soft["pv"]], [],
                                    s_pthi, s_ptlo)
                free["pt"] = state["pt"][1]

            def values():
                def run(e):
                    for m, (a, p) in enumerate(((v_hi, pt_hi), (v_hi, pt_lo), (v_lo, pt_hi))):
                        for b in range(BPT):
                            rows = slice(b * SEQ, (b + 1) * SEQ)
                            last = e.matmul(pv_bank[:, b, 0:256], a[rows, t, j, :], p[rows, :],
                                            start=m == 0, stop=m == 2)
                    return last
                done = PE.do([*state["pt"], *v_marks[t], free["pv"]], run, s_pv)
                soft["pv"] = done
                nonlocal v_read
                v_read = done
                bank = pv_bank[:, :, 0:256].rearrange("p b (h n) -> p b h n", h=GROUP)
                ot_marks[t] = split(bank, ot_hi[:, t, :, :, :].rearrange("p h b n -> p b h n"),
                                    ot_lo[:, t, :, :, :].rearrange("p h b n -> p b h n"),
                                    [done, ot_free[t]], [ot_free[t]], s_othi, s_otlo)
                free["pv"] = ot_marks[t][1]

            later(3, transpose_q)
            later(5, scores)
            later(6, normalise)
            later(8, transpose_p)
            later(10, values)

        soft = {"score": None, "prob": None, "pv": None}
        kt_read = v_read = setup_read

        def width_step(unit, t, b, last_tile, waits, tail=None):
            cols = slice(t * P, (t + 1) * P)
            for c in range(QUARTERS):
                terms = [(act_hi[:, kt, cols], act_lo[:, kt, cols], *unit.wide(kt)) for kt in (2 * c, 2 * c + 1)]
                extra = []
                if c == QUARTERS - 1 and tail is not None:
                    tail_terms, extra = tail()
                    terms += tail_terms
                done = PE.do([main_free[b], *act_marks[t], *unit.marks[c], *waits, *extra],
                             lambda e, c=c, terms=terms: products(e, main_bank[b][:, :], terms, c == 0,
                                                                  c == QUARTERS - 1), s_main)
                if last_tile:
                    slot_free[unit.slot][c] = done
                if c < QUARTERS - 1:
                    tick()
            return done

        def kv_step(blk, pair, t, unit):
            nonlocal n_norm
            b = next_bank()
            done = width_step(unit, t, b, t == TILES - 1, [])
            bank = main_bank[b]
            cols_v = bank[:, 2 * HD:4 * HD].rearrange("p (j n) -> p j n", j=2)
            v_done_hi = AC.do([done, v_read], lambda e: e.activation(v_hi[:, t, :, :], cols_v, ACT.Copy), s_vhi)
            slot = n_norm % 2
            dst, scaled = rms_norm(bank, b, 2, done, [])
            v_done_lo = VE.do([v_done_hi, v_read], lambda e: e.tensor_tensor(
                v_lo[:, t, :, :], cols_v, f32(v_hi[:, t, :, :]), ALU.subtract), s_vlo)
            main_free[b] = v_done_lo
            v_marks[t] = [v_done_hi, v_done_lo]
            gain = kgain[:, :].rearrange("p (o n) -> p o n", o=1).broadcast_to([P, 2, HD])
            d3 = dst[:, 0:2 * HD].rearrange("p (j n) -> p j n", j=2)
            gained = VE.do([scaled, gains], lambda e: e.tensor_tensor(d3, d3, gain, ALU.mult), s_qn)
            later(3, lambda: key_transpose(dst, gained, slot, t))
            tick()

        def q_step(blk, g, t, unit):
            b = next_bank()
            done = width_step(unit, t, b, t == TILES - 1, [])
            act_free[t] = done
            slot = n_norm % 2
            dst, scaled = rms_norm(main_bank[b], b, GROUP, done, [])
            attend(blk, g, t, dst, scaled, slot)
            tick()

        def o_step(blk, g, t, unit):
            for half_no in range(2):
                b = next_bank()
                oc = slice(half_no * WIDE, (half_no + 1) * WIDE)
                for c in range(2):
                    terms = [(ot_hi[:, t, h, :, :].rearrange("p b n -> p (b n)"),
                              ot_lo[:, t, h, :, :].rearrange("p b n -> p (b n)"),
                              unit.hi(h)[:, oc], unit.lo(h)[:, oc]) for h in (2 * c, 2 * c + 1)]
                    marks = [m for h in (2 * c, 2 * c + 1) for m in unit.marks[h]]
                    done = PE.do([main_free[b], *ot_marks[t], *marks],
                                 lambda e, b=b, c=c, terms=terms: products(e, main_bank[b][:, :], terms, c == 0, c == 1),
                                 s_main)
                    if half_no == 1 and t == TILES - 1:
                        for h in (2 * c, 2 * c + 1):
                            slot_free[unit.slot][h] = done
                    if c == 1:
                        main_free[b] = VE.do([done, x_here[t]], lambda e, b=b, oc=oc: e.tensor_tensor(
                            acc[:, t, oc], main_bank[b][:, :], acc[:, t, oc], ALU.add), s_acc)
                        acc_mark[t] = main_free[b]
                    if (half_no, c) != (1, 1):
                        tick()
            ot_free[t] = done
            if g == KV_HEADS - 1:
                later(2, lambda: transpose_x1(t))
                later(6, lambda: low_rank(blk, t))
            tick()

        acc_mark = [None] * TILES
        low_marks = [None] * TILES

        def transpose_x1(t):
            for half_no, (name, bank) in enumerate((("qt", qt_bank), ("s", s_bank))):
                def run(e, half_no=half_no, bank=bank):
                    for k in range(4):
                        kt = 4 * half_no + k
                        last = e.transpose(bank[:, k * P:(k + 1) * P], acc[:, t, kt * P:(kt + 1) * P], ident[:, :])
                    return last
                done = PE.do([acc_mark[t], free[name], const], run, s_tr)
                evacuate_act(t, half_no, name, bank, done)
            acc_mark[t] = PO.do([done, bias_done], lambda e: e.tensor_tensor(
                acc[:, t, :], acc[:, t, :], bias_eff[:, :], ALU.add), s_bias2)

        s_bias2 = sig("s_bias2")
        low_h = qt_hi[:, :, :, :].rearrange("p b h n -> p (b h n)")
        low_l = qt_lo[:, :, :, :].rearrange("p b h n -> p (b h n)")

        def low_rank(blk, t):
            cols = slice(t * P, (t + 1) * P)

            def run(e):
                terms = [(loraa_hi[:, kt, :], loraa_lo[:, kt, :], act_hi[:, kt, cols], act_lo[:, kt, cols])
                         for kt in range(KT)]
                return products(e, pt_bank[:, 0:P], terms, True, True)
            done = PE.do([*act_marks[t], *loraa_marks, free["pt"]], run, s_low)
            first = (blk * TILES + t) * BPT
            chosen = admask[:, first:first + BPT].rearrange("p (b o) -> p b o", o=1).broadcast_to([P, BPT, SEQ])
            masked = VE.do([done, soft["prob"], soft["low"]], lambda e: e.tensor_tensor(
                prob[:, 0:P].rearrange("p (b n) -> p b n", b=BPT),
                pt_bank[:, 0:P].rearrange("p (b n) -> p b n", b=BPT), chosen, ALU.mult), s_lowm)
            free["pt"] = masked
            low_marks[t] = split(prob[:, 0:P], low_h[:, cols], low_l[:, cols], [masked, qt_free[0]], [],
                                 s_lowhi, s_lowlo)
            soft["low"] = low_marks[t][1]

        soft["low"] = None

        def f_step(blk, u, t, unit):
            b = next_bank()
            cols = slice(t * P, (t + 1) * P)
            oc = slice(u * WIDE, (u + 1) * WIDE)

            def tail():
                return [(low_h[:, cols], low_l[:, cols], beff_hi[:, oc], beff_lo[:, oc])], \
                    [*low_marks[t], *beff_marks]
            done = width_step(unit, t, b, t == TILES - 1, [], tail)
            main_free[b] = VE.do([done, acc_mark[t]], lambda e: e.tensor_tensor(
                acc[:, t, oc], main_bank[b][:, :], acc[:, t, oc], ALU.add), s_acc)
            if u == 1:
                act_free[t] = done
                qt_free[0] = done
                stored = PO.do([main_free[b]], lambda e: e.dma_start(out[blk * TILES + t], acc[:, t, :]), s_out[t], 16)
                acc_free[t] = [stored]
                if blk + 1 < BLOCKS:
                    x_here[t] = load_x(blk + 1, t)
            tick()

        for _ in range(2 * UNIT_CHUNKS):
            prepare_next()
        for u, (kind, blk, n) in enumerate(schedule):
            if kind == "kv":
                kt_free = kt_read
                v_free = v_read
                if n == 0:
                    for t in range(TILES):
                        mix(blk, t)
            step = {"kv": kv_step, "q": q_step, "o": o_step, "f": f_step}[kind]
            for t in range(TILES):
                if u > 0:
                    later(1, prepare_next)
                step(blk, n, t, units[u])
        for q in sorted(side):
            for work in side[q]:
                work()
        PO.do([*f_done, *(m for marks in acc_free for m in marks)], lambda e: e.memset(half[:, :], -0.5), s_mset)

        block = ctx.enter_context(nc.Block())

        @block.sync
        def _(eng):
            SP.emit(eng)

        @block.gpsimd
        def _(eng):
            PO.emit(eng)

        @block.scalar
        def _(eng):
            AC.emit(eng)

        @block.vector
        def _(eng):
            VE.emit(eng)

        @block.tensor
        def _(eng):
            PE.emit(eng)


def _wide_units(w, n_units):
    return w.reshape(UNIT_CHUNKS, 2, P, n_units, WIDE).transpose(3, 0, 2, 1, 4).reshape(
        n_units, UNIT_CHUNKS, P, CHUNK)


def _basis():
    n = DM
    at = np.arange(n)
    rows = np.zeros((n, n))
    rows[0] = math.sqrt(n) / n
    f = np.arange(1, (n - 1) // 2 + 1)
    angle = 2 * math.pi * ((f[:, None] * at[None, :]) % n) / n
    rows[1:n - 1:2] = math.sqrt(n / 2.0) * 2 / n * np.cos(angle)
    rows[2:n:2] = math.sqrt(n / 2.0) * 2 / n * np.sin(angle)
    rows[n - 1] = math.sqrt(n) / n * np.where(at % 2 == 0, 1.0, -1.0)
    return rows.astype(np.float32)


def _alibi():
    start = 2 ** (-2 ** (-(math.log2(HEADS) - 3)))
    slopes = np.array([start * start ** i for i in range(HEADS)], dtype=np.float32)
    pos = np.arange(SEQ, dtype=np.float32)
    rel = pos[None, :] - pos[:, None]
    table = np.where(rel > 0, np.float32(-1e30), slopes[:, None, None] * rel).astype(np.float32)
    return table.reshape(HEADS // 2, 2, SEQ, SEQ).transpose(1, 2, 0, 3).reshape(P, HEADS // 2, SEQ)


def kernel(x, itok_B_0_15, itok_B_1_7, L0_cond_weights, L0_attn_Wq, L0_attn_Wk, L0_attn_Wv, L0_attn_Wo,
           L0_attn_q_norm_w, L0_attn_k_norm_w, L0_cond2_weight, L0_cond2_bias, L0_cond2_lora_a_weights,
           L0_cond2_lora_b_weights, L0_cond2_scaling_factors, L0_ffn_W_base, L0_ffn_b_base, L0_ffn_enc0,
           L0_ffn_enc1, L0_ffn_coefs0, L0_ffn_coefs1, L0_ffn_mask0, L0_ffn_mask1):
    import concourse.bacc as bacc
    from concourse.bass_utils import run_bass_kernel_spmd

    A = np.asarray
    wk = A(L0_attn_Wk).reshape(4, 2 * HD, DM)
    wv = A(L0_attn_Wv).reshape(4, 2 * HD, DM)
    wkv = np.concatenate([wk, wv], axis=1).reshape(4 * WIDE, DM)
    coefs = np.concatenate([A(L0_ffn_coefs0), A(L0_ffn_coefs1)], axis=2)
    masks = np.concatenate([A(L0_ffn_mask0), A(L0_ffn_mask1)], axis=2)

    def by_row(a):
        return a.reshape(EXPERTS, KT, P, ENC).transpose(2, 0, 1, 3).reshape(P, EXPERTS * KT * ENC)

    w2 = A(L0_cond2_weight).reshape(KT, P, KT, P).transpose(2, 1, 0, 3).reshape(KT, P, CHUNK)
    lora_b = A(L0_cond2_lora_b_weights).transpose(1, 0, 2).reshape(KT, P, P).transpose(1, 0, 2).reshape(1, P, CHUNK)
    b2 = np.broadcast_to(A(L0_cond2_bias).reshape(KT, P, 1), (KT, P, P)).transpose(1, 0, 2).reshape(1, P, CHUNK)
    host = {
        "x": A(x).reshape(TOKENS // P, P, DM),
        "mix_of_batch": A(itok_B_0_15).reshape(1, BATCH),
        "adapter_of_batch": np.broadcast_to(A(itok_B_1_7).reshape(1, BATCH), (P, BATCH)),
        "adapter_of_row": (np.arange(P) // RANK).astype(np.float32).reshape(P, 1),
        "adapter_scale": np.repeat(A(L0_cond2_scaling_factors), RANK).reshape(P, 1),
        "mix_w": A(L0_cond_weights),
        "wq": _wide_units(A(L0_attn_Wq).T, KV_HEADS),
        "wkv": _wide_units(wkv.T, 4),
        "wo": A(L0_attn_Wo).T.reshape(KV_HEADS, GROUP, HD, DM),
        "q_norm_w": np.broadcast_to(A(L0_attn_q_norm_w), (P, HD)),
        "k_norm_w": np.broadcast_to(A(L0_attn_k_norm_w), (P, HD)),
        "w2_units": np.concatenate([w2, lora_b, b2], axis=0),
        "lora_a": A(L0_cond2_lora_a_weights).reshape(P, KT, P).transpose(2, 1, 0).reshape(P, CHUNK),
        "w_base": _wide_units(A(L0_ffn_W_base).T, 2),
        "b_base": np.broadcast_to(A(L0_ffn_b_base), (P, DM)),
        "encoders": np.concatenate([A(L0_ffn_enc0), A(L0_ffn_enc1)], axis=0),
        "coefs": by_row(coefs),
        "masks": by_row(masks),
        "basis": _wide_units(_basis(), 2),
        "alibi": _alibi(),
        "identity": np.eye(P, dtype=np.float32),
    }
    nc = bacc.Bacc("TRN2", target_bir_lowering=False, num_devices=1)
    arrays, aps = {}, {}
    for name, a in host.items():
        a = np.ascontiguousarray(a)
        arrays[f"in_{name}"] = a
        aps[name] = nc.dram_tensor(f"in_{name}", a.shape, mybir.dt.from_np(a.dtype), kind="ExternalInput").ap()
    out = nc.dram_tensor("out_tokens", (TOKENS // P, P, DM), F32, kind="ExternalOutput").ap()
    build_program(nc, aps, out)
    r = run_bass_kernel_spmd(nc, [arrays], core_ids=[0])
    return r.results[0]["out_tokens"].reshape(BATCH, SEQ, DM)
```

```python
from contextlib import ExitStack
import math

import numpy as np
import concourse.bass as bass
from concourse import mybir

F32 = mybir.dt.float32
F32R = mybir.dt.float32r
I32 = mybir.dt.int32
U8 = mybir.dt.uint8
ALU = mybir.AluOpType
ACT = mybir.ActivationFunctionType
AXIS = mybir.AxisListType

P = 128
BATCH, SEQ, DM = 32, 64, 1024
KT = DM // P
HEADS, KV_HEADS, HD = 32, 8, 128
GROUP = HEADS // KV_HEADS
TOKENS = BATCH * SEQ
BLOCK = 512
TILES = BLOCK // P
BLOCKS = TOKENS // BLOCK
BPT = P // SEQ
WIDE = 512
UNIT_CHUNKS = 4
CHUNK = 1024
RAWS = 3
ADAPTERS, RANK = 8, 16
EXPERTS, ENC = 3, 40
EPS = 1e-6
SCALING = 16.0 / 32.0
AT = dict(square=0.55, mean=0.8, scale=1.9,
          tq=2.6, tq_hi=3.2, tq_lo=3.8,
          s=4, s_add=5.3, s_exp=5.8, s_norm=6,
          tp=7.4, tp_hi=9.1, tp_lo=9.6,
          v=10, v_hi=10.4, v_lo=10.7,
          add=0.6,
          x1=3, low=4.9,
          w_hi=2.1, w_lo=3.7)
QUARTERS = 4


class Signal:

    def __init__(self, handle):
        self.handle, self.count = handle, 0


class Queue:

    def __init__(self):
        self.items = []

    def do(self, waits, build, signal=None, by=1):
        if signal is not None:
            signal.count += by
        self.items.append((list(waits), build, signal, by))
        return None if signal is None else (signal, signal.count)

    def emit(self, eng):
        reached = {}
        for waits, build, signal, by in self.items:
            for mark in waits:
                if mark is not None and reached.get(mark[0], 0) < mark[1]:
                    eng.wait_ge(mark[0].handle, mark[1])
                    reached[mark[0]] = mark[1]
            last = build(eng)
            if signal is not None:
                last.then_inc(signal.handle, by)


def build_program(nc, d, out):
    ctx = ExitStack()
    with ctx:
        def sb(name, shape, dt=F32):
            return ctx.enter_context(nc.sbuf_tensor(name, shape, dt))

        def sig(name):
            return Signal(ctx.enter_context(nc.semaphore(name)))

        ring_hi = sb("ring_hi", [P, 2, UNIT_CHUNKS, CHUNK], F32R)
        ring_lo = sb("ring_lo", [P, 2, UNIT_CHUNKS, CHUNK], F32R)
        act_hi = sb("act_hi", [P, KT, BLOCK], F32R)
        act_lo = sb("act_lo", [P, KT, BLOCK], F32R)
        acc = sb("acc", [P, TILES, DM])
        raw = [sb(f"raw{i}", [P, CHUNK]) for i in range(RAWS)]
        k_t = sb("k_t", [P, 2, BLOCK // SEQ, 2, SEQ], F32R)
        v_hi = sb("v_hi", [P, TILES, 2, HD], F32R)
        v_lo = sb("v_lo", [P, TILES, 2, HD], F32R)
        ot_hi = sb("ot_hi", [P, TILES, GROUP, BPT, SEQ], F32R)
        ot_lo = sb("ot_lo", [P, TILES, GROUP, BPT, SEQ], F32R)
        qn = [sb(f"qn{i}", [P, GROUP * HD]) for i in range(2)]
        sq = sb("sq", [P, GROUP * HD])
        qt_hi = sb("qt_hi", [P, BPT, GROUP, SEQ], F32R)
        qt_lo = sb("qt_lo", [P, BPT, GROUP, SEQ], F32R)
        score = sb("score", [P, 256])
        prob = sb("prob", [P, 256])
        pt_hi = sb("pt_hi", [P, 256], F32R)
        pt_lo = sb("pt_lo", [P, 256], F32R)
        alibi = sb("alibi", [P, HEADS // 2, SEQ])
        beff_hi = sb("beff_hi", [P, DM], F32R)
        beff_lo = sb("beff_lo", [P, DM], F32R)
        bias_eff = sb("bias_eff", [P, DM])
        loraa_hi = sb("loraa_hi", [P, KT, P], F32R)
        loraa_lo = sb("loraa_lo", [P, KT, P], F32R)
        mixw_raw = sb("mixw_raw", [P, TILES, P])
        mixw_hi = sb("mixw_hi", [P, TILES, P], F32R)
        mixw_lo = sb("mixw_lo", [P, TILES, P], F32R)
        ident = sb("ident", [P, P])
        kgain = sb("kgain", [P, HD])
        qgain = sb("qgain", [P, HD])
        mixidx = sb("mixidx", [1, BATCH], I32)
        adidx = sb("adidx", [P, BATCH], I32)
        adidf = sb("adidf", [P, BATCH])
        admask = sb("admask", [P, BATCH])
        adrow = sb("adrow", [P, 1])
        adscale = sb("adscale", [P, 1])
        mask8 = sb("mask8", [P, EXPERTS * KT * ENC], U8)
        half = sb("half", [P, GROUP])
        ssum = sb("ssum", [P, GROUP])
        mean = sb("mean", [P, GROUP])
        rstd = sb("rstd", [P, GROUP])
        peak = sb("peak", [P, 4])
        total = sb("total", [P, 4])
        inv = sb("inv", [P, 4])

        main_bank = [ctx.enter_context(nc.psum_tensor(f"main{i}", [P, WIDE], F32)) for i in range(3)]
        qt_bank = ctx.enter_context(nc.psum_tensor("qt_bank", [P, WIDE], F32))
        s_bank = ctx.enter_context(nc.psum_tensor("s_bank", [P, WIDE], F32))
        pt_bank = ctx.enter_context(nc.psum_tensor("pt_bank", [P, WIDE], F32))
        pv_bank = ctx.enter_context(nc.psum_tensor("pv_bank", [P, BPT, WIDE], F32))
        main_free = [None] * 3
        free = {"qt": None, "s": None, "pt": None, "pv": None}

        f_scratch = nc.dram_tensor("f_scratch", [2, UNIT_CHUNKS, P, 2, WIDE], F32).ap()

        PE, AC, VE, PO, SP = Queue(), Queue(), Queue(), Queue(), Queue()

        s_const = sig("s_const")
        s_coef = sig("s_coef")
        s_raw = [sig(f"s_raw{i}") for i in range(RAWS)]
        s_hi, s_lo = sig("s_hi"), sig("s_lo")
        s_fold = sig("s_fold")
        s_main = sig("s_main")
        s_prep = sig("s_prep")
        s_mset = sig("s_mset")
        s_wc = sig("s_wc")
        s_mixhi, s_mixlo = sig("s_mixhi"), sig("s_mixlo")
        s_x = [sig(f"s_x{t}") for t in range(TILES)]
        s_xhi, s_xlo = sig("s_xhi"), sig("s_xlo")
        s_tr = sig("s_tr")
        s_acthi, s_actlo = sig("s_acthi"), sig("s_actlo")
        s_sq, s_mean, s_rstd, s_qn = (sig(n) for n in ("s_sq", "s_mean", "s_rstd", "s_qn"))
        s_vhi, s_vlo = sig("s_vhi"), sig("s_vlo")
        s_kthi, s_ktlo = sig("s_kthi"), sig("s_ktlo")
        s_qthi, s_qtlo = sig("s_qthi"), sig("s_qtlo")
        s_sc, s_soft, s_exp, s_prob = sig("s_sc"), sig("s_soft"), sig("s_exp"), sig("s_prob")
        s_pt, s_pthi, s_ptlo = sig("s_pt"), sig("s_pthi"), sig("s_ptlo")
        s_pv, s_othi, s_otlo = sig("s_pv"), sig("s_othi"), sig("s_otlo")
        s_acc = sig("s_acc")
        s_bias = sig("s_bias")
        s_low, s_lowm, s_lowhi, s_lowlo = (sig(n) for n in ("s_low", "s_lowm", "s_lowhi", "s_lowlo"))
        s_evac = sig("s_evac")
        s_fst = [sig(f"s_fst{i}") for i in range(4)]
        s_out = [sig(f"s_out{t}") for t in range(TILES)]
        s_idx = sig("s_idx")

        def f32(ap):
            return ap.bitcast(F32)

        def split(src, hi, lo, waits_hi, waits_lo, sig_hi, sig_lo):
            hi_done = AC.do(waits_hi, lambda e: e.activation(hi, src, ACT.Copy), sig_hi)
            lo_done = VE.do([hi_done, *waits_lo],
                            lambda e: e.tensor_tensor(lo, src, f32(hi), ALU.subtract), sig_lo)
            return hi_done, lo_done

        def split_later(base, at_hi, at_lo, src, hi, lo, waits, sig_hi, sig_lo, then):
            def low():
                lo_done = VE.do([marks[0], *waits], lambda e: e.tensor_tensor(lo, src, f32(hi), ALU.subtract), sig_lo)
                then([marks[0], lo_done])
            marks = []
            at(base, at_hi, lambda: marks.append(AC.do(waits, lambda e: e.activation(hi, src, ACT.Copy), sig_hi)))
            at(base, at_lo, low)

        def products(eng, bank, terms, start, stop):
            last = None
            for n, (lh, ll, rh, rl) in enumerate(terms):
                for m, (a, b) in enumerate(((lh, rh), (lh, rl), (ll, rh))):
                    last = eng.matmul(bank, a, b, start=start and n == 0 and m == 0,
                                      stop=stop and n == len(terms) - 1 and m == 2)
            return last

        consts = 0

        def load_const(dst, src):
            nonlocal consts
            consts += 1
            return AC.do([], lambda e: e.dma_start(dst, src), s_const, 16)

        COEF = EXPERTS * KT * ENC
        coef_raw, coef_masked = acc[:, 0, 0:COEF], acc[:, 1, 0:COEF]
        AC.do([], lambda e: e.dma_start(coef_raw, d["coefs"]), s_coef, 16)
        coef_here = AC.do([], lambda e: e.dma_start(mask8[:, :], d["masks"]), s_coef, 16)
        load_const(ident[:, :], d["identity"])
        load_const(alibi[:, :, :], d["alibi"])
        load_const(bias_eff[:, :], d["b_base"])
        load_const(kgain[:, :], d["k_norm_w"])
        load_const(qgain[:, :], d["q_norm_w"])
        load_const(adidx[:, :], d["adapter_of_batch"])
        load_const(adrow[:, :], d["adapter_of_row"])
        load_const(adscale[:, :], d["adapter_scale"])
        const = (s_const, 16 * consts)
        idx_here = SP.do([], lambda e: e.dma_start(mixidx[:, :], d["mix_of_batch"]), s_idx, 16)
        mset = PO.do([], lambda e: e.memset(mixw_raw[:, :, :], 0.0), s_mset)
        mset = PO.do([], lambda e: e.memset(half[:, :], -0.5), s_mset)

        raw_free = [None] * RAWS
        n_raw = 0
        slot_free = [[None] * UNIT_CHUNKS for _ in range(2)]
        n_unit = 0

        def load_raw(src, rows=P, after=()):
            nonlocal n_raw
            i = n_raw % RAWS
            n_raw += 1
            here = SP.do([raw_free[i], *after], lambda e: e.dma_start(raw[i][0:rows, :], src), s_raw[i], 16)
            return i, here

        class Unit:

            def __init__(self, chunks, after=()):
                nonlocal n_unit
                self.slot = n_unit % 2
                n_unit += 1
                self.chunks, self.after = chunks, after
                self.marks = [[] for _ in range(UNIT_CHUNKS)]
                self.rounded = [None] * UNIT_CHUNKS

            def hi(self, c):
                return ring_hi[:, self.slot, c, :]

            def lo(self, c):
                return ring_lo[:, self.slot, c, :]

            def prepare_hi(self, c):
                i, here = load_raw(self.chunks[c], after=self.after)
                self.rounded[c] = i, AC.do([here, slot_free[self.slot][c]], lambda e: e.activation(
                    self.hi(c), raw[i][:, :], ACT.Copy), s_hi)

            def prepare_lo(self, c):
                i, hi_done = self.rounded[c]
                lo_done = VE.do([hi_done, slot_free[self.slot][c]], lambda e: e.tensor_tensor(
                    self.lo(c), raw[i][:, :], f32(self.hi(c)), ALU.subtract), s_lo)
                raw_free[i] = lo_done
                self.marks[c] = [hi_done, lo_done]

            def prepare(self, c):
                self.prepare_hi(c)
                self.prepare_lo(c)

            def wide(self, kt):
                a = (kt % 2) * WIDE
                return self.hi(kt // 2)[:, a:a + WIDE], self.lo(kt // 2)[:, a:a + WIDE]

        W40 = KT * ENC
        mark = VE.do([coef_here], lambda e: e.tensor_tensor(coef_masked, coef_raw, mask8[:, :], ALU.mult), s_prep)
        part = [acc[:, 1, e * W40:(e + 1) * W40] for e in range(EXPERTS)]
        mark = VE.do([mark], lambda e: e.tensor_tensor(coef_raw[:, 0:W40], part[0], part[1], ALU.add), s_prep)
        mark = VE.do([mark], lambda e: e.tensor_tensor(coef_raw[:, W40:2 * W40], coef_raw[:, 0:W40], part[2],
                                                       ALU.add), s_prep)
        mark = VE.do([mark], lambda e: e.tensor_scalar(coef_raw[:, 0:W40], coef_raw[:, W40:2 * W40], SCALING, None,
                                                       ALU.mult), s_prep)
        k_flat = k_t[:, :, :, :, :].rearrange("p a b c n -> p (a b c n)")
        coef_hi, coef_lo = k_flat[:, 0:W40], k_flat[:, W40:2 * W40]
        coef_marks = split(coef_raw[:, 0:W40], coef_hi, coef_lo, [mark], [], s_hi, s_lo)
        enc_hi = v_hi[0:ENC, :, :, :].rearrange("p a b n -> p (a b n)")
        enc_lo = v_lo[0:ENC, :, :, :].rearrange("p a b n -> p (a b n)")
        i, here = load_raw(d["encoders"], rows=ENC)
        enc_marks = split(raw[i][0:ENC, :], enc_hi, enc_lo, [here], [], s_hi, s_lo)
        raw_free[i] = enc_marks[1]

        n_main = 0

        def next_bank():
            nonlocal n_main
            b = n_main % 3
            n_main += 1
            return b

        wt_hi = ot_hi[0:ENC, :, :, :, :].rearrange("p a b c n -> p (a b c n)")[:, 0:DM]
        wt_lo = ot_lo[0:ENC, :, :, :, :].rearrange("p a b c n -> p (a b c n)")[:, 0:DM]
        wt_marks = []
        for u in range(2):
            unit = Unit([d["basis"][u, c] for c in range(UNIT_CHUNKS)])
            b = next_bank()
            for c in range(UNIT_CHUNKS):
                unit.prepare(c)
                terms = [(coef_hi[:, kt * ENC:(kt + 1) * ENC], coef_lo[:, kt * ENC:(kt + 1) * ENC], *unit.wide(kt))
                         for kt in (2 * c, 2 * c + 1)]
                done = PE.do([main_free[b], *coef_marks, *unit.marks[c]],
                             lambda e, b=b, c=c, terms=terms: products(e, main_bank[b][0:ENC, :], terms, c == 0,
                                                                       c == UNIT_CHUNKS - 1), s_main)
                slot_free[unit.slot][c] = done
            cols = slice(u * WIDE, (u + 1) * WIDE)
            marks = split(main_bank[b][0:ENC, :], wt_hi[:, cols], wt_lo[:, cols], [done], [], s_hi, s_lo)
            main_free[b] = marks[1]
            wt_marks.append(marks)

        mark = VE.do([const], lambda e: e.tensor_copy(adidf[:, :], adidx[:, :]), s_prep)
        VE.do([mark], lambda e: e.tensor_scalar(admask[:, :], adidf[:, :], adrow[:, 0:1], adscale[:, 0:1],
                                                ALU.is_equal, ALU.mult), s_prep)
        mark = VE.do([const], lambda e: e.tensor_tensor(kgain[:, :], kgain[:, :], qgain[:, :], ALU.mult), s_prep)
        gains = VE.do([mark], lambda e: e.tensor_scalar(kgain[:, :], kgain[:, :], 1.0 / math.sqrt(HD), None,
                                                        ALU.mult), s_prep)

        mix_free = [None]
        mix_state = {}

        def gather_mix(blk):
            for j in range(TILES * BPT):
                t, b = j // BPT, j % BPT
                dst = mixw_raw[b * SEQ:(b + 1) * SEQ, t, b * SEQ:(b + 1) * SEQ]

                def gather(e, batch=blk * TILES * BPT + j, dst=dst):
                    which = e.value_load(mixidx[0:1, batch:batch + 1], min_val=0, max_val=15)
                    return e.dma_start(dst, d["mix_w"][bass.ds(which, 1), :, :].rearrange("a c n -> (a c) n"))
                here = SP.do([idx_here, mset, mix_state.get("split")], gather, s_wc, 16)
            mix_state["here"] = here

        acc_free = [list(coef_marks) for _ in range(TILES)]

        def load_x(blk, t):
            return PO.do(acc_free[t], lambda e: e.dma_start(acc[:, t, :], d["x"][blk * TILES + t]), s_x[t], 16)

        x_here = [load_x(0, t) for t in range(2)] + [None, None]
        gather_mix(0)

        side = {}
        quarter = [0]

        def at(base, delay, work):
            side.setdefault(base + delay, []).append(work)

        def later(delay, work):
            at(quarter[0], delay, work)

        def tick():
            quarter[0] += 1
            while side and min(side) <= quarter[0]:
                for work in side.pop(min(side)):
                    work()

        schedule = []
        for blk in range(BLOCKS):
            for g in range(KV_HEADS):
                if g % 2 == 0:
                    schedule.append(("kv", blk, g // 2))
                schedule += [("q", blk, g), ("o", blk, g)]
            schedule += [("f", blk, 0), ("f", blk, 1)]
        sources = {"kv": d["wkv"], "q": d["wq"], "o": d["wo"],
                   "f": f_scratch.rearrange("u c p j n -> u c p (j n)")}
        units = {}
        n_prepared = 0
        qt_free = [None]

        def prepare_next():
            nonlocal n_prepared
            u, c = divmod(n_prepared, UNIT_CHUNKS)
            if u >= len(schedule):
                return lambda: None
            kind, blk, n = schedule[u]
            if c == 0:
                if kind == "kv" and n == 0 and blk > 0:
                    gather_mix(blk)
                units[u] = Unit([sources[kind][n, j] for j in range(UNIT_CHUNKS)],
                                after=f_done if kind == "f" else ())
            n_prepared += 1
            units[u].prepare_hi(c)
            return lambda: units[u].prepare_lo(c)

        f_done = [None] * 4
        act_marks = [None] * TILES
        act_free = [None] * TILES
        ot_free = [None] * TILES

        def x_halves(t):
            r = 2 * (t % 2)
            return [o[:, r:r + 2, :, :, :].rearrange("p a h b n -> p (a h b n)") for o in (ot_hi, ot_lo)]

        def mix_split(t):
            if t == 0:
                mix_state["marks"] = split(mixw_raw[:, :, :], mixw_hi[:, :, :], mixw_lo[:, :, :],
                                           [mix_state["here"], mix_free[0]], [mix_free[0]], s_mixhi, s_mixlo)
                mix_state["split"] = mix_state["marks"][1]
            xh, xl = x_halves(t)
            r = 2 * (t % 2)
            mix_state[t] = split(acc[:, t, :], xh, xl, [x_here[t], ot_free[r], ot_free[r + 1]], [], s_xhi, s_xlo)

        def mix_products(t):
            xh, xl = x_halves(t)
            for half_no, (name, bank) in enumerate((("qt", qt_bank), ("s", s_bank))):
                def run(e, half_no=half_no, bank=bank):
                    for k in range(4):
                        kt = 4 * half_no + k
                        term = (xh[:, kt * P:(kt + 1) * P], xl[:, kt * P:(kt + 1) * P],
                                mixw_hi[:, t, :], mixw_lo[:, t, :])
                        last = products(e, bank[:, k * P:(k + 1) * P], [term], True, True)
                    return last
                done = PE.do([free[name], *mix_state[t], *mix_state["marks"]], run, s_tr)
                evacuate_act(t, half_no, name, bank, done)
            mix_free[0] = done
            r = 2 * (t % 2)
            ot_free[r] = ot_free[r + 1] = done

        def evacuate_act(t, half_no, name, bank, done):
            dst_h = act_hi[:, 4 * half_no:4 * half_no + 4, t * P:(t + 1) * P]
            dst_l = act_lo[:, 4 * half_no:4 * half_no + 4, t * P:(t + 1) * P]
            src = bank[:, :].rearrange("p (k n) -> p k n", k=4)
            marks = split(src, dst_h, dst_l, [done, act_free[t]], [], s_acthi, s_actlo)
            free[name] = marks[1]
            act_marks[t] = marks

        weff = [Unit(None), Unit(None)]

        def weff_chunk(u, c):
            unit = weff[u]
            cols = slice(u * WIDE, (u + 1) * WIDE)
            i, here = load_raw(d["w_base"][u, c])
            for j in range(2):
                kt = 2 * c + j
                b = next_bank()
                rows = slice(kt * P, (kt + 1) * P)
                term = (enc_hi[:, rows], enc_lo[:, rows], wt_hi[:, cols], wt_lo[:, cols])
                done = PE.do([main_free[b], *enc_marks, *wt_marks[u]],
                             lambda e, b=b, term=term: products(e, main_bank[b][:, :], [term], True, True), s_main)
                folded = add_bank(b, raw[i][:, j * WIDE:(j + 1) * WIDE], [here, done], s_fold)
            f = slot_free[unit.slot][c]
            unit.marks[c] = split(raw[i][:, :], unit.hi(c), unit.lo(c), [folded, f], [f], s_hi, s_lo)
            raw_free[i] = unit.marks[c][1]
            for t in range(TILES):
                ot_free[t] = done

        def add_bank(b, dst, waits, signal):
            main_free[b] = VE.do(waits, lambda e: e.tensor_tensor(dst, main_bank[b][:, :], dst, ALU.add), signal)
            return main_free[b]

        B_UNIT, BIAS_UNIT = KT, KT + 1
        n_store = 0
        part_of = [(u + 2) % TILES for u in range(KT + 2)]
        stationary = {}

        def split_stationary(n):
            q = part_of[n]
            i, here = load_raw(d["w2_units"][n])
            cols = slice(q * P, (q + 1) * P)
            stationary[n] = split(raw[i][:, :].rearrange("p (k n) -> p k n", k=KT), act_hi[:, :, cols],
                                  act_lo[:, :, cols], [here, act_free[q]], [act_free[q]], s_hi, s_lo)
            raw_free[i] = stationary[n][1]

        def weff_product(n, u):
            nonlocal n_store, beff_marks, bias_done
            b = next_bank()
            q = part_of[n]
            cols = slice(q * P, (q + 1) * P)
            for c in range(UNIT_CHUNKS):
                terms = [(act_hi[:, kt, cols], act_lo[:, kt, cols], *weff[u].wide(kt)) for kt in (2 * c, 2 * c + 1)]
                done = PE.do([main_free[b], *stationary[n], *weff[u].marks[c]],
                             lambda e, c=c, terms=terms: products(e, main_bank[b][:, :], terms, c == 0,
                                                                  c == UNIT_CHUNKS - 1), s_main)
                slot_free[weff[u].slot][c] = done
            act_free[q] = done
            oc = slice(u * WIDE, (u + 1) * WIDE)
            if n < KT:
                st = n_store % 4
                n_store += 1
                stage = acc[:, 2 + st // 2, (st % 2) * WIDE:(st % 2 + 1) * WIDE]
                main_free[b] = AC.do([done, f_done[st]], lambda e: e.activation(
                    stage, main_bank[b][:, :], ACT.Copy), s_evac)
                f_done[st] = PO.do([main_free[b]], lambda e: e.dma_start(f_scratch[u, n // 2, :, n % 2, :], stage),
                                   s_fst[st], 16)
            elif n == B_UNIT:
                beff_marks = split(main_bank[b][:, :], beff_hi[:, oc], beff_lo[:, oc], [done], [], s_hi, s_lo)
                main_free[b] = beff_marks[1]
            else:
                bias_done = add_bank(b, bias_eff[:, oc], [done, const], s_bias)

        beff_marks = bias_done = None
        split_stationary(0)
        for c in range(UNIT_CHUNKS):
            weff_chunk(0, c)
        split_stationary(1)
        weff_product(0, 0)
        weff_chunk(1, 0)
        weff_chunk(1, 1)
        weff_product(1, 0)
        weff_chunk(1, 2)
        weff_chunk(1, 3)
        split_stationary(2)
        weff_product(0, 1)
        split_stationary(3)
        weff_product(1, 1)
        for n in range(2, KT):
            split_stationary(n + 2)
            weff_product(n, 0)
            weff_product(n, 1)
            if n == 3:
                i, here = load_raw(d["lora_a"])
                loraa_marks = split(raw[i][:, :].rearrange("p (k n) -> p k n", k=KT), loraa_hi[:, :, :],
                                    loraa_lo[:, :, :], [here], [], s_hi, s_lo)
                raw_free[i] = loraa_marks[1]
        mix_split(0)
        weff_product(B_UNIT, 0)
        mix_split(1)
        weff_product(BIAS_UNIT, 0)
        for _ in range(UNIT_CHUNKS):
            prepare_next()()
        weff_product(B_UNIT, 1)
        mix_products(0)
        weff_product(BIAS_UNIT, 1)
        for t in (2, 3):
            acc_free[t] = list(f_done)
            x_here[t] = load_x(0, t)
        mix_split(2)
        mix_products(1)
        for _ in range(UNIT_CHUNKS):
            prepare_next()()
        setup_read = slot_free[weff[1].slot][UNIT_CHUNKS - 1]
        kt_free = v_free = setup_read

        n_norm = 0

        def rms_norm(bank, b, heads, done, squares_done, then):
            nonlocal n_norm
            slot = n_norm % 2
            n_norm += 1
            dst = qn[slot]
            w = heads * HD
            state = {}

            def square():
                def run(e):
                    for h in range(heads):
                        last = e.activation(sq[:, h * HD:(h + 1) * HD], bank[:, h * HD:(h + 1) * HD], ACT.Square,
                                            accum_out=ssum[:, h:h + 1])
                    return last
                state["sq"] = AC.do([done, sum_state["mean"]], run, s_sq)

            def average():
                averaged = VE.do([state["sq"], sum_state["rstd"]], lambda e: e.tensor_scalar(
                    mean[:, 0:heads], ssum[:, 0:heads], 1.0 / HD, EPS, ALU.mult, ALU.add), s_mean)
                sum_state["mean"] = averaged
                sum_state["rstd"] = PO.do([averaged, mset, sum_state["qn"]], lambda e: e.tensor_tensor(
                    rstd[:, 0:heads], mean[:, 0:heads], half[:, 0:heads], ALU.pow), s_rstd)
                squares_done(state["sq"])

            def scale():
                scaled = VE.do([sum_state["rstd"], state["sq"], qn_free[slot]], lambda e: e.tensor_tensor(
                    dst[:, 0:w].rearrange("p (h n) -> p h n", h=heads),
                    bank[:, 0:w].rearrange("p (h n) -> p h n", h=heads),
                    rstd[:, 0:heads].rearrange("p (h o) -> p h o", o=1).broadcast_to([P, heads, HD]), ALU.mult), s_qn)
                sum_state["qn"] = scaled
                main_free[b] = scaled
                then(dst, scaled, slot)
            later(AT["square"], square)
            later(AT["mean"], average)
            later(AT["scale"], scale)

        sum_state = {"mean": None, "rstd": None, "qn": None}
        qn_free = [None, None]

        def key_transpose(base, src, ready, slot, t):
            def run(e):
                for j in range(2):
                    last = e.transpose(qt_bank[:, j * P:(j + 1) * P], src[:, j * P:(j + 1) * P], ident[:, :])
                return last
            done = PE.do([ready, free["qt"], const], run, s_tr)
            qn_free[slot] = done
            batches = slice(t * BPT, (t + 1) * BPT)

            def evacuated(marks):
                free["qt"] = marks[1]
                kt_marks[t] = marks
            split_later(base, AT["tq_hi"], AT["tq_lo"], qt_bank[:, 0:2 * P].rearrange("p (j b n) -> p j b n", j=2, b=BPT),
                        k_t[:, :, batches, 0, :], k_t[:, :, batches, 1, :], [done, kt_free], s_kthi, s_ktlo, evacuated)

        kt_marks = [None] * TILES
        v_marks = [None] * TILES
        ot_marks = [None] * TILES

        def attend(base, g, t, src, ready, slot):
            j = g % 2
            state = {}

            def transpose_q():
                def run(e):
                    for h in range(GROUP):
                        last = e.transpose(qt_bank[:, h * P:(h + 1) * P], src[:, h * P:(h + 1) * P], ident[:, :])
                    return last
                done = PE.do([ready, free["qt"], const], run, s_tr)
                qn_free[slot] = done

                def evacuated(marks):
                    state["qt"] = marks
                    free["qt"] = marks[1]
                split_later(base, AT["tq_hi"], AT["tq_lo"],
                            qt_bank[:, :].rearrange("p (h b n) -> p h b n", h=GROUP, b=BPT),
                            qt_hi[:, :, :, :].rearrange("p b h n -> p h b n"),
                            qt_lo[:, :, :, :].rearrange("p b h n -> p h b n"),
                            [done, qt_free[0]], s_qthi, s_qtlo, evacuated)

            def scores():
                def run(e):
                    for hp in range(2):
                        for b in range(BPT):
                            a = (hp * BPT + b) * 2 * SEQ
                            lh = qt_hi[:, b, 2 * hp:2 * hp + 2, :].rearrange("p h n -> p (h n)")
                            ll = qt_lo[:, b, 2 * hp:2 * hp + 2, :].rearrange("p h n -> p (h n)")
                            keys = k_t[:, j, t * BPT + b, :, :].rearrange("p c n -> p (c n)")
                            e.matmul(s_bank[:, a:a + 2 * SEQ], lh, keys, start=True, stop=False)
                            last = e.matmul(s_bank[:, a:a + SEQ], ll, keys[:, 0:SEQ], start=False, stop=True)
                    return last
                nonlocal kt_read
                state["s"] = kt_read = qt_free[0] = PE.do([*state["qt"], *kt_marks[t], free["s"]], run, s_sc)

            def bias_and_peak():
                parts = s_bank[:, :].rearrange("p (h b c n) -> p h b c n", h=2, b=BPT, c=2)
                table = alibi[:, 2 * g:2 * g + 2, :].rearrange("p h (o n) -> p h o n", o=1)\
                    .broadcast_to([P, 2, BPT, SEQ])
                rows = score[:, :].rearrange("p (h b n) -> p h b n", h=2, b=BPT)
                biased = VE.do([state["s"], const, soft["score"]], lambda e: e.tensor_tensor(
                    rows, parts[:, :, :, 0, :], table, ALU.add), s_soft)
                biased = VE.do([biased], lambda e: e.tensor_tensor(rows, parts[:, :, :, 1, :], rows, ALU.add), s_soft)
                free["s"] = biased
                by_row = score[:, :].rearrange("p (r n) -> p r n", n=SEQ)
                peaked = VE.do([biased], lambda e: e.tensor_reduce(peak[:, :], by_row, AXIS.X, ALU.max), s_soft)
                state["shifted"] = VE.do([peaked], lambda e: e.tensor_tensor(
                    by_row, by_row, peak[:, :].rearrange("p (r o) -> p r o", o=1).broadcast_to([P, 4, SEQ]),
                    ALU.subtract), s_soft)

            def exponential():
                soft["score"] = state["exp"] = AC.do([state["shifted"], soft["prob"]], lambda e: e.activation(
                    prob[:, :], score[:, :], ACT.Exp), s_exp)

            def normalise():
                p_row = prob[:, :].rearrange("p (r n) -> p r n", n=SEQ)
                summed = VE.do([state["exp"]], lambda e: e.tensor_reduce(total[:, :], p_row, AXIS.X, ALU.add), s_soft)
                inverse = VE.do([summed], lambda e: e.reciprocal(inv[:, :], total[:, :]), s_soft)
                state["prob"] = VE.do([inverse], lambda e: e.tensor_tensor(
                    p_row, p_row, inv[:, :].rearrange("p (r o) -> p r o", o=1).broadcast_to([P, 4, SEQ]),
                    ALU.mult), s_prob)

            def transpose_p():
                def run(e):
                    for hp in range(2):
                        last = e.transpose(pt_bank[:, hp * P:(hp + 1) * P], prob[:, hp * P:(hp + 1) * P], ident[:, :])
                    return last
                done = PE.do([state["prob"], free["pt"], const], run, s_pt)
                soft["prob"] = done

                def evacuated(marks):
                    state["pt"] = marks
                    free["pt"] = marks[1]
                split_later(base, AT["tp_hi"], AT["tp_lo"], pt_bank[:, 0:256], pt_hi[:, :], pt_lo[:, :],
                            [done, soft["pv"]], s_pthi, s_ptlo, evacuated)

            def values():
                def run(e):
                    for m, (a, p) in enumerate(((v_hi, pt_hi), (v_hi, pt_lo), (v_lo, pt_hi))):
                        for b in range(BPT):
                            rows = slice(b * SEQ, (b + 1) * SEQ)
                            last = e.matmul(pv_bank[:, b, 0:256], a[rows, t, j, :], p[rows, :],
                                            start=m == 0, stop=m == 2)
                    return last
                nonlocal v_read
                done = soft["pv"] = v_read = PE.do([*state["pt"], *v_marks[t], free["pv"]], run, s_pv)

                def evacuated(marks):
                    ot_marks[t] = marks
                    free["pv"] = marks[1]
                split_later(base, AT["v_hi"], AT["v_lo"],
                            pv_bank[:, :, 0:256].rearrange("p b (h n) -> p b h n", h=GROUP),
                            ot_hi[:, t, :, :, :].rearrange("p h b n -> p b h n"),
                            ot_lo[:, t, :, :, :].rearrange("p h b n -> p b h n"),
                            [done, ot_free[t]], s_othi, s_otlo, evacuated)

            for when, work in (("tq", transpose_q), ("s", scores), ("s_add", bias_and_peak), ("s_exp", exponential),
                               ("s_norm", normalise), ("tp", transpose_p), ("v", values)):
                at(base, AT[when], work)

        soft = {"score": None, "prob": None, "pv": None}
        kt_read = v_read = setup_read

        def width_step(unit, t, b, last_tile, waits, tail=None):
            cols = slice(t * P, (t + 1) * P)
            for c in range(QUARTERS):
                terms = [(act_hi[:, kt, cols], act_lo[:, kt, cols], *unit.wide(kt)) for kt in (2 * c, 2 * c + 1)]
                extra = []
                if c == QUARTERS - 1 and tail is not None:
                    tail_terms, extra = tail()
                    terms += tail_terms
                done = PE.do([main_free[b], *act_marks[t], *unit.marks[c], *waits, *extra],
                             lambda e, c=c, terms=terms: products(e, main_bank[b][:, :], terms, c == 0,
                                                                  c == QUARTERS - 1), s_main)
                if last_tile:
                    slot_free[unit.slot][c] = done
                if c < QUARTERS - 1:
                    tick()
            return done

        def kv_step(blk, pair, t, unit):
            b = next_bank()
            done = width_step(unit, t, b, t == TILES - 1, [])
            tick()
            base = quarter[0]
            bank = main_bank[b]
            cols_v = bank[:, 2 * HD:4 * HD].rearrange("p (j n) -> p j n", j=2)
            v_done_hi = AC.do([done, v_read], lambda e: e.activation(v_hi[:, t, :, :], cols_v, ACT.Copy), s_vhi)

            def low_half_of_v(squared):
                v_marks[t] = [v_done_hi, VE.do([v_done_hi, squared, v_read], lambda e: e.tensor_tensor(
                    v_lo[:, t, :, :], cols_v, f32(v_hi[:, t, :, :]), ALU.subtract), s_vlo)]

            def gain_and_transpose(dst, scaled, slot):
                gain = kgain[:, :].rearrange("p (o n) -> p o n", o=1).broadcast_to([P, 2, HD])
                d3 = dst[:, 0:2 * HD].rearrange("p (j n) -> p j n", j=2)
                gained = VE.do([scaled, gains], lambda e: e.tensor_tensor(d3, d3, gain, ALU.mult), s_qn)
                at(base, AT["tq"], lambda: key_transpose(base, dst, gained, slot, t))
            rms_norm(bank, b, 2, done, low_half_of_v, gain_and_transpose)

        def q_step(blk, g, t, unit):
            b = next_bank()
            done = width_step(unit, t, b, t == TILES - 1, [])
            act_free[t] = done
            tick()
            base = quarter[0]
            rms_norm(main_bank[b], b, GROUP, done, lambda squared: None,
                     lambda dst, scaled, slot: attend(base, g, t, dst, scaled, slot))

        def o_step(blk, g, t, unit):
            for half_no in range(2):
                b = next_bank()
                oc = slice(half_no * WIDE, (half_no + 1) * WIDE)
                for c in range(2):
                    terms = [(ot_hi[:, t, h, :, :].rearrange("p b n -> p (b n)"),
                              ot_lo[:, t, h, :, :].rearrange("p b n -> p (b n)"),
                              unit.hi(h)[:, oc], unit.lo(h)[:, oc]) for h in (2 * c, 2 * c + 1)]
                    marks = [m for h in (2 * c, 2 * c + 1) for m in unit.marks[h]]
                    done = PE.do([main_free[b], *ot_marks[t], *marks],
                                 lambda e, b=b, c=c, terms=terms: products(e, main_bank[b][:, :], terms, c == 0, c == 1),
                                 s_main)
                    if half_no == 1 and t == TILES - 1:
                        for h in (2 * c, 2 * c + 1):
                            slot_free[unit.slot][h] = done
                    tick()

                def accumulate(b=b, oc=oc, done=done):
                    main_free[b] = VE.do([done, x_here[t]], lambda e: e.tensor_tensor(
                        acc[:, t, oc], main_bank[b][:, :], acc[:, t, oc], ALU.add), s_acc)
                    acc_mark[t] = main_free[b]
                later(AT["add"], accumulate)
            ot_free[t] = done
            if g == KV_HEADS - 1:
                later(AT["x1"], lambda: transpose_x1(t))
                if t % 2 == 1:
                    later(AT["low"], lambda: low_rank(blk, t // 2))

        acc_mark = [None] * TILES
        low_marks = [None] * TILES

        def transpose_x1(t):
            for half_no, (name, bank) in enumerate((("qt", qt_bank), ("s", s_bank))):
                def run(e, half_no=half_no, bank=bank):
                    for k in range(4):
                        kt = 4 * half_no + k
                        last = e.transpose(bank[:, k * P:(k + 1) * P], acc[:, t, kt * P:(kt + 1) * P], ident[:, :])
                    return last
                done = PE.do([acc_mark[t], free[name], const], run, s_tr)
                evacuate_act(t, half_no, name, bank, done)
            acc_mark[t] = PO.do([done, bias_done], lambda e: e.tensor_tensor(
                acc[:, t, :], acc[:, t, :], bias_eff[:, :], ALU.add), s_bias2)

        s_bias2 = sig("s_bias2")
        low_h = qt_hi[:, :, :, :].rearrange("p b h n -> p (b h n)")
        low_l = qt_lo[:, :, :, :].rearrange("p b h n -> p (b h n)")

        def low_rank(blk, pair):
            n_batch = 2 * BPT
            cols = slice(2 * pair * P, (2 * pair + 2) * P)

            def run(e):
                terms = [(loraa_hi[:, kt, :], loraa_lo[:, kt, :], act_hi[:, kt, cols], act_lo[:, kt, cols])
                         for kt in range(KT)]
                return products(e, pt_bank[:, 0:2 * P], terms, True, True)
            done = PE.do([*act_marks[2 * pair], *act_marks[2 * pair + 1], *loraa_marks, free["pt"]], run, s_low)
            first = blk * TILES * BPT + pair * n_batch
            chosen = admask[:, first:first + n_batch].rearrange("p (b o) -> p b o", o=1)\
                .broadcast_to([P, n_batch, SEQ])
            masked = VE.do([done, soft["prob"], soft["low"]], lambda e: e.tensor_tensor(
                prob[:, :].rearrange("p (b n) -> p b n", b=n_batch),
                pt_bank[:, 0:2 * P].rearrange("p (b n) -> p b n", b=n_batch), chosen, ALU.mult), s_lowm)
            free["pt"] = masked
            marks = split(prob[:, :], low_h[:, cols], low_l[:, cols], [masked, qt_free[0]], [], s_lowhi, s_lowlo)
            low_marks[2 * pair] = low_marks[2 * pair + 1] = marks
            soft["low"] = marks[1]

        soft["low"] = None

        def f_step(blk, u, t, unit):
            b = next_bank()
            cols = slice(t * P, (t + 1) * P)
            oc = slice(u * WIDE, (u + 1) * WIDE)

            def tail():
                return [(low_h[:, cols], low_l[:, cols], beff_hi[:, oc], beff_lo[:, oc])], \
                    [*low_marks[t], *beff_marks]
            done = width_step(unit, t, b, t == TILES - 1, [], tail)
            tick()
            if u == 1:
                act_free[t] = done
                qt_free[0] = done

            def finish():
                main_free[b] = VE.do([done, acc_mark[t]], lambda e: e.tensor_tensor(
                    acc[:, t, oc], main_bank[b][:, :], acc[:, t, oc], ALU.add), s_acc)
                if u == 1:
                    stored = PO.do([main_free[b]], lambda e: e.dma_start(out[blk * TILES + t], acc[:, t, :]),
                                   s_out[t], 16)
                    acc_free[t] = [stored]
                    if blk + 1 < BLOCKS:
                        later(2, reload)

            def reload():
                x_here[t] = load_x(blk + 1, t)
            later(AT["add"], finish)
            if u == 1 and blk + 1 < BLOCKS:
                later(8, lambda: mix_split(t))
                later(10, lambda: mix_products(t))

        def prepare_ahead():
            later(AT["w_lo"] - AT["w_hi"], prepare_next())

        for u, (kind, blk, n) in enumerate(schedule):
            if kind == "kv":
                kt_free = kt_read
                v_free = v_read
            step = {"kv": kv_step, "q": q_step, "o": o_step, "f": f_step}[kind]
            for t in range(TILES):
                if u > 0:
                    later(AT["w_hi"], prepare_ahead)
                if (kind, blk, n) == ("kv", 0, 0) and t >= 2:
                    mix_products(t)
                if (kind, blk, n, t) == ("kv", 0, 0, 0):
                    mix_split(3)
                step(blk, n, t, units[u])
        while side:
            tick()
        PO.do([*f_done, *(m for marks in acc_free for m in marks)], lambda e: e.memset(half[:, :], -0.5), s_mset)

        block = ctx.enter_context(nc.Block())

        @block.sync
        def _(eng):
            SP.emit(eng)

        @block.gpsimd
        def _(eng):
            PO.emit(eng)

        @block.scalar
        def _(eng):
            AC.emit(eng)

        @block.vector
        def _(eng):
            VE.emit(eng)

        @block.tensor
        def _(eng):
            PE.emit(eng)


def _wide_units(w, n_units):
    return w.reshape(UNIT_CHUNKS, 2, P, n_units, WIDE).transpose(3, 0, 2, 1, 4).reshape(
        n_units, UNIT_CHUNKS, P, CHUNK)


def _basis():
    n = DM
    at = np.arange(n)
    rows = np.zeros((n, n))
    rows[0] = math.sqrt(n) / n
    f = np.arange(1, (n - 1) // 2 + 1)
    angle = 2 * math.pi * ((f[:, None] * at[None, :]) % n) / n
    rows[1:n - 1:2] = math.sqrt(n / 2.0) * 2 / n * np.cos(angle)
    rows[2:n:2] = math.sqrt(n / 2.0) * 2 / n * np.sin(angle)
    rows[n - 1] = math.sqrt(n) / n * np.where(at % 2 == 0, 1.0, -1.0)
    return rows.astype(np.float32)


def _alibi():
    start = 2 ** (-2 ** (-(math.log2(HEADS) - 3)))
    slopes = np.array([start * start ** i for i in range(HEADS)], dtype=np.float32)
    pos = np.arange(SEQ, dtype=np.float32)
    rel = pos[None, :] - pos[:, None]
    table = np.where(rel > 0, np.float32(-1e30), slopes[:, None, None] * rel).astype(np.float32)
    return table.reshape(HEADS // 2, 2, SEQ, SEQ).transpose(1, 2, 0, 3).reshape(P, HEADS // 2, SEQ)


def kernel(x, itok_B_0_15, itok_B_1_7, L0_cond_weights, L0_attn_Wq, L0_attn_Wk, L0_attn_Wv, L0_attn_Wo,
           L0_attn_q_norm_w, L0_attn_k_norm_w, L0_cond2_weight, L0_cond2_bias, L0_cond2_lora_a_weights,
           L0_cond2_lora_b_weights, L0_cond2_scaling_factors, L0_ffn_W_base, L0_ffn_b_base, L0_ffn_enc0,
           L0_ffn_enc1, L0_ffn_coefs0, L0_ffn_coefs1, L0_ffn_mask0, L0_ffn_mask1):
    import concourse.bacc as bacc
    from concourse.bass_utils import run_bass_kernel_spmd

    A = np.asarray
    wk = A(L0_attn_Wk).reshape(4, 2 * HD, DM)
    wv = A(L0_attn_Wv).reshape(4, 2 * HD, DM)
    wkv = np.concatenate([wk, wv], axis=1).reshape(4 * WIDE, DM)
    coefs = np.concatenate([A(L0_ffn_coefs0), A(L0_ffn_coefs1)], axis=2)
    masks = np.concatenate([A(L0_ffn_mask0), A(L0_ffn_mask1)], axis=2)

    def by_row(a):
        return a.reshape(EXPERTS, KT, P, ENC).transpose(2, 0, 1, 3).reshape(P, EXPERTS * KT * ENC)

    w2 = A(L0_cond2_weight).reshape(KT, P, KT, P).transpose(2, 1, 0, 3).reshape(KT, P, CHUNK)
    lora_b = A(L0_cond2_lora_b_weights).transpose(1, 0, 2).reshape(KT, P, P).transpose(1, 0, 2).reshape(1, P, CHUNK)
    b2 = np.broadcast_to(A(L0_cond2_bias).reshape(KT, P, 1), (KT, P, P)).transpose(1, 0, 2).reshape(1, P, CHUNK)
    host = {
        "x": A(x).reshape(TOKENS // P, P, DM),
        "mix_of_batch": A(itok_B_0_15).reshape(1, BATCH),
        "adapter_of_batch": np.broadcast_to(A(itok_B_1_7).reshape(1, BATCH), (P, BATCH)),
        "adapter_of_row": (np.arange(P) // RANK).astype(np.float32).reshape(P, 1),
        "adapter_scale": np.repeat(A(L0_cond2_scaling_factors), RANK).reshape(P, 1),
        "mix_w": A(L0_cond_weights),
        "wq": _wide_units(A(L0_attn_Wq).T, KV_HEADS),
        "wkv": _wide_units(wkv.T, 4),
        "wo": A(L0_attn_Wo).T.reshape(KV_HEADS, GROUP, HD, DM),
        "q_norm_w": np.broadcast_to(A(L0_attn_q_norm_w), (P, HD)),
        "k_norm_w": np.broadcast_to(A(L0_attn_k_norm_w), (P, HD)),
        "w2_units": np.concatenate([w2, lora_b, b2], axis=0),
        "lora_a": A(L0_cond2_lora_a_weights).reshape(P, KT, P).transpose(2, 1, 0).reshape(P, CHUNK),
        "w_base": _wide_units(A(L0_ffn_W_base).T, 2),
        "b_base": np.broadcast_to(A(L0_ffn_b_base), (P, DM)),
        "encoders": np.concatenate([A(L0_ffn_enc0), A(L0_ffn_enc1)], axis=0),
        "coefs": by_row(coefs),
        "masks": by_row(masks),
        "basis": _wide_units(_basis(), 2),
        "alibi": _alibi(),
        "identity": np.eye(P, dtype=np.float32),
    }
    nc = bacc.Bacc("TRN2", target_bir_lowering=False, num_devices=1)
    arrays, aps = {}, {}
    for name, a in host.items():
        a = np.ascontiguousarray(a)
        arrays[f"in_{name}"] = a
        aps[name] = nc.dram_tensor(f"in_{name}", a.shape, mybir.dt.from_np(a.dtype), kind="ExternalInput").ap()
    out = nc.dram_tensor("out_tokens", (TOKENS // P, P, DM), F32, kind="ExternalOutput").ap()
    build_program(nc, aps, out)
    r = run_bass_kernel_spmd(nc, [arrays], core_ids=[0])
    return r.results[0]["out_tokens"].reshape(BATCH, SEQ, DM)
```

```python
from contextlib import ExitStack
import math

import numpy as np
import concourse.bass as bass
from concourse import mybir

F32 = mybir.dt.float32
F32R = mybir.dt.float32r
I32 = mybir.dt.int32
U8 = mybir.dt.uint8
ALU = mybir.AluOpType
ACT = mybir.ActivationFunctionType
AXIS = mybir.AxisListType

P = 128
BATCH, SEQ, DM = 32, 64, 1024
KT = DM // P
HEADS, KV_HEADS, HD = 32, 8, 128
GROUP = HEADS // KV_HEADS
TOKENS = BATCH * SEQ
BLOCK = 512
TILES = BLOCK // P
BLOCKS = TOKENS // BLOCK
BPT = P // SEQ
WIDE = 512
UNIT_CHUNKS = 4
CHUNK = 1024
RAWS = 3
ADAPTERS, RANK = 8, 16
EXPERTS, ENC = 3, 40
EPS = 1e-6
SCALING = 16.0 / 32.0
AT = dict(square=0.15, mean=1.3, scale=1.7,
          tq=2.8, tq_hi=3.4, tq_lo=3.9,
          s=4.8, s_add=5.5, s_exp=6.3, s_norm=6.4,
          tp=7.9, tp_hi=8, tp_lo=8.6,
          v=10, v_hi=10.7, v_lo=11.3,
          add=1.6,
          mix_split=7.4, mix=9.8, reload=5.1,
          x1=4.9, low=7.2,
          w_hi=1.2, w_lo=3.8)
assert AT["add"] < AT["x1"] < AT["low"] < 8 and AT["tq_lo"] < 4 and AT["v_lo"] < 12
assert AT["add"] < AT["reload"] < AT["mix_split"] < AT["mix"] < 12
QUARTERS = 4


class Signal:

    def __init__(self, handle):
        self.handle, self.count = handle, 0


class Queue:

    def __init__(self):
        self.items = []

    def do(self, waits, build, signal=None, by=1):
        if signal is not None:
            signal.count += by
        self.items.append((list(waits), build, signal, by))
        return None if signal is None else (signal, signal.count)

    def emit(self, eng):
        reached = {}
        for waits, build, signal, by in self.items:
            for mark in waits:
                if mark is not None and reached.get(mark[0], 0) < mark[1]:
                    eng.wait_ge(mark[0].handle, mark[1])
                    reached[mark[0]] = mark[1]
            last = build(eng)
            if signal is not None:
                last.then_inc(signal.handle, by)


def build_program(nc, d, out):
    ctx = ExitStack()
    with ctx:
        def sb(name, shape, dt=F32):
            return ctx.enter_context(nc.sbuf_tensor(name, shape, dt))

        def sig(name):
            return Signal(ctx.enter_context(nc.semaphore(name)))

        ring_hi = sb("ring_hi", [P, 2, UNIT_CHUNKS, CHUNK], F32R)
        ring_lo = sb("ring_lo", [P, 2, UNIT_CHUNKS, CHUNK], F32R)
        act_hi = sb("act_hi", [P, KT, BLOCK], F32R)
        act_lo = sb("act_lo", [P, KT, BLOCK], F32R)
        acc = sb("acc", [P, TILES, DM])
        raw = [sb(f"raw{i}", [P, CHUNK]) for i in range(RAWS)]
        k_t = sb("k_t", [P, 2, BLOCK // SEQ, 2, SEQ], F32R)
        v_hi = sb("v_hi", [P, TILES, 2, HD], F32R)
        v_lo = sb("v_lo", [P, TILES, 2, HD], F32R)
        ot_hi = sb("ot_hi", [P, TILES, GROUP, BPT, SEQ], F32R)
        ot_lo = sb("ot_lo", [P, TILES, GROUP, BPT, SEQ], F32R)
        qn = [sb(f"qn{i}", [P, GROUP * HD]) for i in range(2)]
        sq = sb("sq", [P, GROUP * HD])
        qt_hi = sb("qt_hi", [P, BPT, GROUP, SEQ], F32R)
        qt_lo = sb("qt_lo", [P, BPT, GROUP, SEQ], F32R)
        score = sb("score", [P, 256])
        prob = sb("prob", [P, 256])
        pt_hi = sb("pt_hi", [P, 256], F32R)
        pt_lo = sb("pt_lo", [P, 256], F32R)
        alibi = sb("alibi", [P, HEADS // 2, SEQ])
        beff_hi = sb("beff_hi", [P, DM], F32R)
        beff_lo = sb("beff_lo", [P, DM], F32R)
        bias_eff = sb("bias_eff", [P, DM])
        loraa_hi = sb("loraa_hi", [P, KT, P], F32R)
        loraa_lo = sb("loraa_lo", [P, KT, P], F32R)
        mixw_raw = sb("mixw_raw", [P, TILES, P])
        mixw_hi = sb("mixw_hi", [P, TILES, P], F32R)
        mixw_lo = sb("mixw_lo", [P, TILES, P], F32R)
        ident = sb("ident", [P, P])
        kgain = sb("kgain", [P, HD])
        qgain = sb("qgain", [P, HD])
        mixidx = sb("mixidx", [1, BATCH], I32)
        adidx = sb("adidx", [P, BATCH], I32)
        adidf = sb("adidf", [P, BATCH])
        admask = sb("admask", [P, BATCH])
        adrow = sb("adrow", [P, 1])
        adscale = sb("adscale", [P, 1])
        mask8 = sb("mask8", [P, EXPERTS * KT * ENC], U8)
        half = sb("half", [P, GROUP])
        b2 = sb("b2", [P, KT])
        ssum = sb("ssum", [P, GROUP])
        mean = sb("mean", [P, GROUP])
        rstd = sb("rstd", [P, GROUP])
        peak = sb("peak", [P, 4])
        total = sb("total", [P, 4])
        inv = sb("inv", [P, 4])

        main_bank = [ctx.enter_context(nc.psum_tensor(f"main{i}", [P, WIDE], F32)) for i in range(3)]
        qt_bank = ctx.enter_context(nc.psum_tensor("qt_bank", [P, WIDE], F32))
        s_bank = ctx.enter_context(nc.psum_tensor("s_bank", [P, WIDE], F32))
        pt_bank = ctx.enter_context(nc.psum_tensor("pt_bank", [P, WIDE], F32))
        pv_bank = ctx.enter_context(nc.psum_tensor("pv_bank", [P, BPT, WIDE], F32))
        main_free = [None] * 3
        free = {"qt": None, "s": None, "pt": None, "pv": None}

        f_scratch = nc.dram_tensor("f_scratch", [2, UNIT_CHUNKS, P, 2, WIDE], F32).ap()

        PE, AC, VE, PO, SP = Queue(), Queue(), Queue(), Queue(), Queue()

        s_const = sig("s_const")
        s_coef = sig("s_coef")
        s_raw = [sig(f"s_raw{i}") for i in range(RAWS + 2)]
        s_hi, s_lo = sig("s_hi"), sig("s_lo")
        s_bsum = sig("s_bsum")
        s_fold = sig("s_fold")
        s_main = sig("s_main")
        s_prep = sig("s_prep")
        s_mset = sig("s_mset")
        s_wc = sig("s_wc")
        s_mixhi, s_mixlo = sig("s_mixhi"), sig("s_mixlo")
        s_x = [sig(f"s_x{t}") for t in range(TILES)]
        s_xhi, s_xlo = sig("s_xhi"), sig("s_xlo")
        s_tr = sig("s_tr")
        s_acthi, s_actlo = sig("s_acthi"), sig("s_actlo")
        s_sq, s_mean, s_rstd, s_qn = (sig(n) for n in ("s_sq", "s_mean", "s_rstd", "s_qn"))
        s_vhi, s_vlo = sig("s_vhi"), sig("s_vlo")
        s_kthi, s_ktlo = sig("s_kthi"), sig("s_ktlo")
        s_qthi, s_qtlo = sig("s_qthi"), sig("s_qtlo")
        s_sc, s_soft, s_exp, s_prob = sig("s_sc"), sig("s_soft"), sig("s_exp"), sig("s_prob")
        s_pt, s_pthi, s_ptlo = sig("s_pt"), sig("s_pthi"), sig("s_ptlo")
        s_pv, s_othi, s_otlo = sig("s_pv"), sig("s_othi"), sig("s_otlo")
        s_acc = sig("s_acc")
        s_bias = sig("s_bias")
        s_low, s_lowm, s_lowhi, s_lowlo = (sig(n) for n in ("s_low", "s_lowm", "s_lowhi", "s_lowlo"))
        s_evac = sig("s_evac")
        s_first = [sig(f"s_first{n}") for n in range(2)]
        s_fst = [sig(f"s_fst{i}") for i in range(4)]
        s_out = [sig(f"s_out{t}") for t in range(TILES)]
        s_idx = sig("s_idx")

        def f32(ap):
            return ap.bitcast(F32)

        def split(src, hi, lo, waits_hi, waits_lo, sig_hi, sig_lo):
            hi_done = AC.do(waits_hi, lambda e: e.activation(hi, src, ACT.Copy), sig_hi)
            lo_done = VE.do([hi_done, *waits_lo],
                            lambda e: e.tensor_tensor(lo, src, f32(hi), ALU.subtract), sig_lo)
            return hi_done, lo_done

        def split_later(base, at_hi, at_lo, src, hi, lo, waits, sig_hi, sig_lo, then):
            def low():
                lo_done = VE.do([marks[0], *waits], lambda e: e.tensor_tensor(lo, src, f32(hi), ALU.subtract), sig_lo)
                then([marks[0], lo_done])
            marks = []
            at(base, at_hi, lambda: marks.append(AC.do(waits, lambda e: e.activation(hi, src, ACT.Copy), sig_hi)))
            at(base, at_lo, low)

        def products(eng, bank, terms, start, stop):
            last = None
            for n, (lh, ll, rh, rl) in enumerate(terms):
                for m, (a, b) in enumerate(((lh, rh), (lh, rl), (ll, rh))):
                    last = eng.matmul(bank, a, b, start=start and n == 0 and m == 0,
                                      stop=stop and n == len(terms) - 1 and m == 2)
            return last

        def load_constants():
            def load_const(dst, src):
                return AC.do([], lambda e: e.dma_start(dst, src), s_const, 16)
            load_const(ident[:, :], d["identity"])
            load_const(alibi[:, :, :], d["alibi"])
            load_const(bias_eff[:, :], d["b_base"])
            load_const(kgain[:, :], d["k_norm_w"])
            load_const(qgain[:, :], d["q_norm_w"])
            load_const(b2[:, :], d["b2"])
            load_const(adidx[:, :], d["adapter_of_batch"])
            load_const(adrow[:, :], d["adapter_of_row"])
            return load_const(adscale[:, :], d["adapter_scale"])

        COEF = EXPERTS * KT * ENC
        coef_raw, coef_masked = acc[:, 0, 0:COEF], acc[:, 1, 0:COEF]
        AC.do([], lambda e: e.dma_start(coef_raw, d["coefs"]), s_coef, 16)
        coef_here = AC.do([], lambda e: e.dma_start(mask8[:, :], d["masks"]), s_coef, 16)
        idx_here = SP.do([], lambda e: e.dma_start(mixidx[:, :], d["mix_of_batch"]), s_idx, 16)
        mset = PO.do([], lambda e: e.memset(mixw_raw[:, :, :], 0.0), s_mset)
        mset = PO.do([], lambda e: e.memset(half[:, :], -0.5), s_mset)

        raw = [r[:, :] for r in raw] + [acc[:, t, :] for t in (0, 1)]
        raw_free = [None] * len(raw)
        raws_used = len(raw)
        n_raw = 0
        slot_free = [[None] * UNIT_CHUNKS for _ in range(2)]
        n_unit = 0

        def load_raw(src, rows=P, after=()):
            nonlocal n_raw
            i = n_raw % raws_used
            n_raw += 1
            here = SP.do([raw_free[i], *after], lambda e: e.dma_start(raw[i][0:rows, :], src), s_raw[i], 16)
            return i, here

        class Unit:

            def __init__(self, chunks, after=()):
                nonlocal n_unit
                self.slot = n_unit % 2
                n_unit += 1
                self.chunks, self.after = chunks, after
                self.marks = [[] for _ in range(UNIT_CHUNKS)]
                self.rounded = [None] * UNIT_CHUNKS

            def hi(self, c):
                return ring_hi[:, self.slot, c, :]

            def lo(self, c):
                return ring_lo[:, self.slot, c, :]

            def prepare_hi(self, c):
                i, here = load_raw(self.chunks[c], after=self.after)
                self.rounded[c] = i, AC.do([here, slot_free[self.slot][c]], lambda e: e.activation(
                    self.hi(c), raw[i][:, :], ACT.Copy), s_hi)

            def prepare_lo(self, c):
                i, hi_done = self.rounded[c]
                lo_done = VE.do([hi_done, slot_free[self.slot][c]], lambda e: e.tensor_tensor(
                    self.lo(c), raw[i][:, :], f32(self.hi(c)), ALU.subtract), s_lo)
                raw_free[i] = lo_done
                self.marks[c] = [hi_done, lo_done]

            def prepare(self, c):
                self.prepare_hi(c)
                self.prepare_lo(c)

            def wide(self, kt):
                a = (kt % 2) * WIDE
                return self.hi(kt // 2)[:, a:a + WIDE], self.lo(kt // 2)[:, a:a + WIDE]

        W40 = KT * ENC
        mark = VE.do([coef_here], lambda e: e.tensor_tensor(coef_masked, coef_raw, mask8[:, :], ALU.mult), s_prep)
        part = [acc[:, 1, e * W40:(e + 1) * W40] for e in range(EXPERTS)]
        mark = VE.do([mark], lambda e: e.tensor_tensor(coef_raw[:, 0:W40], part[0], part[1], ALU.add), s_prep)
        mark = VE.do([mark], lambda e: e.tensor_tensor(coef_raw[:, W40:2 * W40], coef_raw[:, 0:W40], part[2],
                                                       ALU.add), s_prep)
        mark = VE.do([mark], lambda e: e.tensor_scalar(coef_raw[:, 0:W40], coef_raw[:, W40:2 * W40], SCALING, None,
                                                       ALU.mult), s_prep)
        k_flat = k_t[:, :, :, :, :].rearrange("p a b c n -> p (a b c n)")
        coef_hi, coef_lo = k_flat[:, 0:W40], k_flat[:, W40:2 * W40]
        coef_marks = split(coef_raw[:, 0:W40], coef_hi, coef_lo, [mark], [], s_hi, s_lo)
        raw_free[RAWS] = raw_free[RAWS + 1] = coef_marks[1]

        enc_hi = v_hi[0:ENC, :, :, :].rearrange("p a b n -> p (a b n)")
        enc_lo = v_lo[0:ENC, :, :, :].rearrange("p a b n -> p (a b n)")
        i, here = load_raw(d["encoders"], rows=ENC)
        enc_marks = split(raw[i][0:ENC, :], enc_hi, enc_lo, [here], [], s_hi, s_lo)
        raw_free[i] = enc_marks[1]

        n_main = 0

        def next_bank():
            nonlocal n_main
            b = n_main % 3
            n_main += 1
            return b

        mix_free = [None]
        mix_state = {}

        def gather_mix(blk):
            for j in range(TILES * BPT):
                t, b = j // BPT, j % BPT
                dst = mixw_raw[b * SEQ:(b + 1) * SEQ, t, b * SEQ:(b + 1) * SEQ]

                def gather(e, batch=blk * TILES * BPT + j, dst=dst):
                    which = e.value_load(mixidx[0:1, batch:batch + 1], min_val=0, max_val=15)
                    return e.dma_start(dst, d["mix_w"][bass.ds(which, 1), :, :].rearrange("a c n -> (a c) n"))
                here = SP.do([idx_here, mset, mix_state.get("split")], gather, s_wc, 16)
            mix_state["here"] = here

        acc_free = [[] for _ in range(TILES)]

        def load_x(blk, t):
            return PO.do(acc_free[t], lambda e: e.dma_start(acc[:, t, :], d["x"][blk * TILES + t]), s_x[t], 16)

        x_here = [None] * TILES

        side = {}
        quarter = [0]

        def at(base, delay, work):
            side.setdefault(base + delay, []).append(work)

        def later(delay, work):
            at(quarter[0], delay, work)

        def tick():
            quarter[0] += 1
            while side and min(side) <= quarter[0]:
                for work in side.pop(min(side)):
                    work()

        schedule = []
        for blk in range(BLOCKS):
            for g in range(KV_HEADS):
                if g % 2 == 0:
                    schedule.append(("kv", blk, g // 2))
                schedule += [("q", blk, g), ("o", blk, g)]
            schedule += [("f", blk, 0), ("f", blk, 1)]
        sources = {"kv": d["wkv"], "q": d["wq"], "o": d["wo"],
                   "f": f_scratch.rearrange("u c p j n -> u c p (j n)")}
        units = {}
        n_prepared = 0
        qt_free = [None]

        def prepare_next():
            nonlocal n_prepared
            u, c = divmod(n_prepared, UNIT_CHUNKS)
            if u >= len(schedule):
                return lambda: None
            kind, blk, n = schedule[u]
            if c == 0:
                if kind == "kv" and n == 0 and blk > 0:
                    gather_mix(blk)
                units[u] = Unit([sources[kind][n, j] for j in range(UNIT_CHUNKS)],
                                after=f_done if kind == "f" else ())
            n_prepared += 1
            units[u].prepare_hi(c)
            return lambda: units[u].prepare_lo(c)

        f_done = [None] * 4
        act_marks = [None] * TILES
        act_free = [None] * TILES
        ot_free = [None] * TILES

        def x_halves(t):
            r = 2 * (t % 2)
            return [o[:, r:r + 2, :, :, :].rearrange("p a h b n -> p (a h b n)") for o in (ot_hi, ot_lo)]

        def mix_split(t):
            if t == 0:
                mix_state["marks"] = split(mixw_raw[:, :, :], mixw_hi[:, :, :], mixw_lo[:, :, :],
                                           [mix_state["here"], mix_free[0]], [mix_free[0]], s_mixhi, s_mixlo)
                mix_state["split"] = mix_state["marks"][1]
            xh, xl = x_halves(t)
            r = 2 * (t % 2)
            mix_state[t] = split(acc[:, t, :], xh, xl, [x_here[t], ot_free[r], ot_free[r + 1]], [], s_xhi, s_xlo)

        def mix_products(t):
            xh, xl = x_halves(t)
            for half_no, (name, bank) in enumerate((("qt", qt_bank), ("s", s_bank))):
                def run(e, half_no=half_no, bank=bank):
                    for k in range(4):
                        kt = 4 * half_no + k
                        term = (xh[:, kt * P:(kt + 1) * P], xl[:, kt * P:(kt + 1) * P],
                                mixw_hi[:, t, :], mixw_lo[:, t, :])
                        last = products(e, bank[:, k * P:(k + 1) * P], [term], True, True)
                    return last
                done = PE.do([free[name], *mix_state[t], *mix_state["marks"]], run, s_tr)
                evacuate_act(t, half_no, name, bank, done)
            mix_free[0] = done
            r = 2 * (t % 2)
            ot_free[r] = ot_free[r + 1] = done

        def evacuate_act(t, half_no, name, bank, done):
            dst_h = act_hi[:, 4 * half_no:4 * half_no + 4, t * P:(t + 1) * P]
            dst_l = act_lo[:, 4 * half_no:4 * half_no + 4, t * P:(t + 1) * P]
            src = bank[:, :].rearrange("p (k n) -> p k n", k=4)
            marks = split(src, dst_h, dst_l, [done, act_free[t]], [], s_acthi, s_actlo)
            free[name] = marks[1]
            act_marks[t] = marks

        basis = Unit([d["basis"][0, c] for c in range(UNIT_CHUNKS)])
        weff = [Unit(None), Unit(None)]

        def weff_chunk(u, c):
            unit = weff[u]
            cols = slice(u * WIDE, (u + 1) * WIDE)
            i, here = load_raw(d["w_base"][u, c])
            for j in range(2):
                kt = 2 * c + j
                b = next_bank()
                rows = slice(kt * P, (kt + 1) * P)
                term = (enc_hi[:, rows], enc_lo[:, rows], wt_hi[:, cols], wt_lo[:, cols])
                done = PE.do([main_free[b], *enc_marks, *wt_marks[u]],
                             lambda e, b=b, term=term: products(e, main_bank[b][:, :], [term], True, True), s_main)
                folded = add_bank(b, raw[i][:, j * WIDE:(j + 1) * WIDE], [here, done], s_fold)
            unit.rounded[c] = i, AC.do([folded, slot_free[unit.slot][c]], lambda e: e.activation(
                unit.hi(c), raw[i][:, :], ACT.Copy), s_hi)
            for t in range(TILES):
                ot_free[t] = done
            return lambda: unit.prepare_lo(c)

        def add_bank(b, dst, waits, signal):
            main_free[b] = VE.do(waits, lambda e: e.tensor_tensor(dst, main_bank[b][:, :], dst, ALU.add), signal)
            return main_free[b]

        B_UNIT = KT
        n_store = 0
        part_of = [(u + 2) % TILES for u in range(KT + 1)]
        stationary = {}

        def split_stationary(n):
            q = part_of[n]
            cols = slice(q * P, (q + 1) * P)
            if n < 2:
                src = acc[:, 2 + n, :]
                here = SP.do([], lambda e: e.dma_start(src, d["w2_units"][n]), s_first[n], 16)
            else:
                i, here = load_raw(d["w2_units"][n])
                src = raw[i]
            stationary[n] = split(src.rearrange("p (k n) -> p k n", k=KT), act_hi[:, :, cols],
                                  act_lo[:, :, cols], [here, act_free[q]], [act_free[q]], s_hi, s_lo)
            if n < 2:
                f_done[2 * n] = f_done[2 * n + 1] = stationary[n][1]
            else:
                raw_free[i] = stationary[n][1]

        def weff_product(n, u):
            nonlocal n_store, beff_marks
            b = next_bank()
            q = part_of[n]
            cols = slice(q * P, (q + 1) * P)
            for c in range(UNIT_CHUNKS):
                terms = [(act_hi[:, kt, cols], act_lo[:, kt, cols], *weff[u].wide(kt)) for kt in (2 * c, 2 * c + 1)]
                done = PE.do([main_free[b], *stationary[n], *weff[u].marks[c]],
                             lambda e, c=c, terms=terms: products(e, main_bank[b][:, :], terms, c == 0,
                                                                  c == UNIT_CHUNKS - 1), s_main)
                slot_free[weff[u].slot][c] = done
            act_free[q] = done
            oc = slice(u * WIDE, (u + 1) * WIDE)
            if n < KT:
                st = n_store % 4
                n_store += 1
                stage = acc[:, 2 + st // 2, (st % 2) * WIDE:(st % 2 + 1) * WIDE]
                main_free[b] = AC.do([done, f_done[st]], lambda e: e.activation(
                    stage, main_bank[b][:, :], ACT.Copy), s_evac)
                f_done[st] = PO.do([main_free[b]], lambda e: e.dma_start(f_scratch[u, n // 2, :, n % 2, :], stage),
                                   s_fst[st], 16)
            else:
                beff_marks = split(main_bank[b][:, :], beff_hi[:, oc], beff_lo[:, oc], [done], [], s_hi, s_lo)
                main_free[b] = beff_marks[1]

        ones_f, ones = prob[:, 0:P], pt_hi[:, 0:P]
        ones_set = PO.do([], lambda e: e.memset(ones_f, 1.0), s_mset)
        ones_done = AC.do([ones_set], lambda e: e.activation(ones, ones_f, ACT.Copy), s_hi)
        bias_sum = [None, None]

        def bias_terms(c):
            for kt in (2 * c, 2 * c + 1):
                for part_no in range(2):
                    for u in range(2):
                        w = f32(weff[u].wide(kt)[part_no])
                        waits = [const, *weff[u].marks[c], bias_sum[u]]
                        if bias_sum[u] is None:
                            def run(e, w=w, u=u):
                                return e.tensor_scalar(qn[u][:, :], w, b2[:, 0:1], None, ALU.mult)
                        else:
                            def run(e, w=w, u=u, kt=kt):
                                return e.scalar_tensor_tensor(qn[u][:, :], w, b2[:, kt:kt + 1], qn[u][:, :],
                                                              ALU.mult, ALU.add)
                        bias_sum[u] = VE.do(waits, run, s_bsum)

        bias_parts = k_flat.rearrange("p (u s n) -> p u s n", u=2, s=2)
        bias_marks = [None, None]

        def bias_split(u):
            bias_marks[u] = split(qn[u][:, :], bias_parts[:, u, 0, :], bias_parts[:, u, 1, :], [bias_sum[u]], [],
                                  s_hi, s_lo)
            qn_free[u] = bias_marks[u][1]

        def bias_product(u):
            b = next_bank()

            def run(e):
                e.matmul(main_bank[b][:, :], ones, bias_parts[:, u, 0, :], start=True, stop=False)
                return e.matmul(main_bank[b][:, :], ones, bias_parts[:, u, 1, :], start=False, stop=True)
            bias_read[0] = PE.do([main_free[b], *bias_marks[u], ones_done], run, s_main)
            return add_bank(b, bias_eff[:, u * WIDE:(u + 1) * WIDE], [bias_read[0], const], s_bias)

        bias_read = [None]
        qn_free = [None, None]

        beff_marks = None

        wt_hi = ot_hi[0:ENC, :, :, :, :].rearrange("p a b c n -> p (a b c n)")[:, 0:DM]
        wt_lo = ot_lo[0:ENC, :, :, :, :].rearrange("p a b c n -> p (a b c n)")[:, 0:DM]
        even_odd = []
        for parity in range(2):
            b = next_bank()
            for c in (2 * parity, 2 * parity + 1):
                basis.prepare(c)
                terms = [(coef_hi[:, kt * ENC:(kt + 1) * ENC], coef_lo[:, kt * ENC:(kt + 1) * ENC], *basis.wide(kt))
                         for kt in (2 * c, 2 * c + 1)]
                done = PE.do([main_free[b], *coef_marks, *basis.marks[c]],
                             lambda e, b=b, c=c, terms=terms: products(e, main_bank[b][0:ENC, :], terms, c % 2 == 0,
                                                                       c % 2 == 1), s_main)
                slot_free[basis.slot][c] = done
            even_odd.append((b, done))
        split_stationary(0)
        split_stationary(1)
        (even_bank, even_done), (odd_bank, odd_done) = even_odd
        even = sq[0:ENC, :]
        main_free[even_bank] = AC.do([even_done], lambda e: e.activation(
            even, main_bank[even_bank][0:ENC, :], ACT.Copy), s_evac)
        wt_marks = []
        for u, op in enumerate((ALU.add, ALU.subtract)):
            wt = qn[u][0:ENC, :]
            main_free[odd_bank] = VE.do([main_free[even_bank], odd_done], lambda e, wt=wt, op=op: e.tensor_tensor(
                wt, even, main_bank[odd_bank][0:ENC, :], op), s_prep)
            cols = slice(u * WIDE, (u + 1) * WIDE)
            wt_marks.append(split(wt, wt_hi[:, cols], wt_lo[:, cols], [main_free[odd_bank]], [], s_hi, s_lo))

        low = [weff_chunk(0, 0)]
        for c in range(1, UNIT_CHUNKS):
            low.append(weff_chunk(0, c))
            low.pop(0)()
        low.pop()()
        weff_product(0, 0)
        low = weff_chunk(1, 0)
        split_stationary(2)
        low()
        weff_product(1, 0)
        low = weff_chunk(1, 1)
        split_stationary(3)
        low()
        weff_product(2, 0)
        const = load_constants()
        gather_mix(0)
        low = weff_chunk(1, 2)
        low()
        weff_product(3, 0)
        low = weff_chunk(1, 3)
        low()
        for n in range(KT):
            if n == KT - 1:
                bias_product(0)
                bias_done = bias_product(1)
            if n >= 4:
                weff_product(n, 0)
            weff_product(n, 1)
            if n + 4 <= B_UNIT:
                split_stationary(n + 4)
            if n == 4:
                raws_used = RAWS
                for t in (0, 1):
                    acc_free[t] = [raw_free[RAWS + t]]
                    x_here[t] = load_x(0, t)
            if 1 <= n <= UNIT_CHUNKS:
                bias_terms(n - 1)
            if n == 5:
                mix_split(0)
                bias_split(0)
                bias_split(1)
            if n == 6:
                mix_split(1)
                i, here = load_raw(d["lora_a"])
                loraa_marks = split(raw[i][:, :].rearrange("p (k n) -> p k n", k=KT), loraa_hi[:, :, :],
                                    loraa_lo[:, :, :], [here], [], s_hi, s_lo)
                raw_free[i] = loraa_marks[1]
        mark = VE.do([const], lambda e: e.tensor_copy(adidf[:, :], adidx[:, :]), s_prep)
        VE.do([mark], lambda e: e.tensor_scalar(admask[:, :], adidf[:, :], adrow[:, 0:1], adscale[:, 0:1],
                                                ALU.is_equal, ALU.mult), s_prep)
        mark = VE.do([const], lambda e: e.tensor_tensor(kgain[:, :], kgain[:, :], qgain[:, :], ALU.mult), s_prep)
        gains = VE.do([mark], lambda e: e.tensor_scalar(kgain[:, :], kgain[:, :], 1.0 / math.sqrt(HD), None,
                                                        ALU.mult), s_prep)

        for t in (2, 3):
            acc_free[t] = list(f_done)
            x_here[t] = load_x(0, t)
        weff_product(B_UNIT, 0)
        prepare_next()()
        mix_products(0)
        prepare_next()()
        prepare_next()()
        mix_split(2)
        prepare_next()()
        weff_product(B_UNIT, 1)
        mix_products(1)
        for _ in range(UNIT_CHUNKS):
            prepare_next()()
        setup_read = slot_free[weff[1].slot][UNIT_CHUNKS - 1]
        kt_free = v_free = setup_read

        n_norm = 0

        def rms_norm(bank, b, heads, done, squares_done, then):
            nonlocal n_norm
            slot = n_norm % 2
            n_norm += 1
            dst = qn[slot]
            w = heads * HD
            state = {}

            def square():
                def run(e):
                    for h in range(heads):
                        last = e.activation(sq[:, h * HD:(h + 1) * HD], bank[:, h * HD:(h + 1) * HD], ACT.Square,
                                            accum_out=ssum[:, h:h + 1])
                    return last
                state["sq"] = AC.do([done, sum_state["mean"]], run, s_sq)

            def average():
                averaged = VE.do([state["sq"], sum_state["rstd"]], lambda e: e.tensor_scalar(
                    mean[:, 0:heads], ssum[:, 0:heads], 1.0 / HD, EPS, ALU.mult, ALU.add), s_mean)
                sum_state["mean"] = averaged
                sum_state["rstd"] = PO.do([averaged, mset, sum_state["qn"]], lambda e: e.tensor_tensor(
                    rstd[:, 0:heads], mean[:, 0:heads], half[:, 0:heads], ALU.pow), s_rstd)
                squares_done(state["sq"])

            def scale():
                scaled = VE.do([sum_state["rstd"], state["sq"], qn_free[slot]], lambda e: e.tensor_tensor(
                    dst[:, 0:w].rearrange("p (h n) -> p h n", h=heads),
                    bank[:, 0:w].rearrange("p (h n) -> p h n", h=heads),
                    rstd[:, 0:heads].rearrange("p (h o) -> p h o", o=1).broadcast_to([P, heads, HD]), ALU.mult), s_qn)
                sum_state["qn"] = scaled
                main_free[b] = scaled
                then(dst, scaled, slot)
            later(AT["square"], square)
            later(AT["mean"], average)
            later(AT["scale"], scale)

        sum_state = {"mean": None, "rstd": None, "qn": None}
        def key_transpose(base, src, ready, slot, t):
            def run(e):
                for j in range(2):
                    last = e.transpose(qt_bank[:, j * P:(j + 1) * P], src[:, j * P:(j + 1) * P], ident[:, :])
                return last
            done = PE.do([ready, free["qt"], const], run, s_tr)
            qn_free[slot] = done
            batches = slice(t * BPT, (t + 1) * BPT)

            def evacuated(marks):
                free["qt"] = marks[1]
                kt_marks[t] = marks
            split_later(base, AT["tq_hi"], AT["tq_lo"],
                        qt_bank[:, 0:2 * P].rearrange("p (j b n) -> p j b n", j=2, b=BPT),
                        k_t[:, :, batches, 0, :], k_t[:, :, batches, 1, :], [done, kt_free], s_kthi, s_ktlo, evacuated)

        kt_marks = [None] * TILES
        v_marks = [None] * TILES
        ot_marks = [None] * TILES

        def attend(base, g, t, src, ready, slot):
            j = g % 2
            state = {}

            def transpose_q():
                def run(e):
                    for h in range(GROUP):
                        last = e.transpose(qt_bank[:, h * P:(h + 1) * P], src[:, h * P:(h + 1) * P], ident[:, :])
                    return last
                done = PE.do([ready, free["qt"], const], run, s_tr)
                qn_free[slot] = done

                def evacuated(marks):
                    state["qt"] = marks
                    free["qt"] = marks[1]
                split_later(base, AT["tq_hi"], AT["tq_lo"],
                            qt_bank[:, :].rearrange("p (h b n) -> p h b n", h=GROUP, b=BPT),
                            qt_hi[:, :, :, :].rearrange("p b h n -> p h b n"),
                            qt_lo[:, :, :, :].rearrange("p b h n -> p h b n"),
                            [done, qt_free[0]], s_qthi, s_qtlo, evacuated)

            def scores():
                def run(e):
                    for hp in range(2):
                        for b in range(BPT):
                            a = (hp * BPT + b) * 2 * SEQ
                            lh = qt_hi[:, b, 2 * hp:2 * hp + 2, :].rearrange("p h n -> p (h n)")
                            ll = qt_lo[:, b, 2 * hp:2 * hp + 2, :].rearrange("p h n -> p (h n)")
                            keys = k_t[:, j, t * BPT + b, :, :].rearrange("p c n -> p (c n)")
                            e.matmul(s_bank[:, a:a + 2 * SEQ], lh, keys, start=True, stop=False)
                            last = e.matmul(s_bank[:, a:a + SEQ], ll, keys[:, 0:SEQ], start=False, stop=True)
                    return last
                nonlocal kt_read
                state["s"] = kt_read = qt_free[0] = PE.do([*state["qt"], *kt_marks[t], free["s"]], run, s_sc)

            def bias_and_peak():
                parts = s_bank[:, :].rearrange("p (h b c n) -> p h b c n", h=2, b=BPT, c=2)
                table = alibi[:, 2 * g:2 * g + 2, :].rearrange("p h (o n) -> p h o n", o=1)\
                    .broadcast_to([P, 2, BPT, SEQ])
                rows = score[:, :].rearrange("p (h b n) -> p h b n", h=2, b=BPT)
                biased = VE.do([state["s"], const, soft["score"]], lambda e: e.tensor_tensor(
                    rows, parts[:, :, :, 0, :], table, ALU.add), s_soft)
                biased = VE.do([biased], lambda e: e.tensor_tensor(rows, parts[:, :, :, 1, :], rows, ALU.add), s_soft)
                free["s"] = biased
                by_row = score[:, :].rearrange("p (r n) -> p r n", n=SEQ)
                peaked = VE.do([biased], lambda e: e.tensor_reduce(peak[:, :], by_row, AXIS.X, ALU.max), s_soft)
                state["shifted"] = VE.do([peaked], lambda e: e.tensor_tensor(
                    by_row, by_row, peak[:, :].rearrange("p (r o) -> p r o", o=1).broadcast_to([P, 4, SEQ]),
                    ALU.subtract), s_soft)

            def exponential():
                soft["score"] = state["exp"] = AC.do([state["shifted"], soft["prob"]], lambda e: e.activation(
                    prob[:, :], score[:, :], ACT.Exp), s_exp)

            def normalise():
                p_row = prob[:, :].rearrange("p (r n) -> p r n", n=SEQ)
                summed = VE.do([state["exp"]], lambda e: e.tensor_reduce(total[:, :], p_row, AXIS.X, ALU.add), s_soft)
                inverse = VE.do([summed], lambda e: e.reciprocal(inv[:, :], total[:, :]), s_soft)
                state["prob"] = VE.do([inverse], lambda e: e.tensor_tensor(
                    p_row, p_row, inv[:, :].rearrange("p (r o) -> p r o", o=1).broadcast_to([P, 4, SEQ]),
                    ALU.mult), s_prob)

            def transpose_p():
                def run(e):
                    for hp in range(2):
                        last = e.transpose(pt_bank[:, hp * P:(hp + 1) * P], prob[:, hp * P:(hp + 1) * P], ident[:, :])
                    return last
                done = PE.do([state["prob"], free["pt"], const], run, s_pt)
                soft["prob"] = done

                def evacuated(marks):
                    state["pt"] = marks
                    free["pt"] = marks[1]
                split_later(base, AT["tp_hi"], AT["tp_lo"], pt_bank[:, 0:256], pt_hi[:, :], pt_lo[:, :],
                            [done, soft["pv"]], s_pthi, s_ptlo, evacuated)

            def values():
                def run(e):
                    for m, (a, p) in enumerate(((v_hi, pt_hi), (v_hi, pt_lo), (v_lo, pt_hi))):
                        for b in range(BPT):
                            rows = slice(b * SEQ, (b + 1) * SEQ)
                            last = e.matmul(pv_bank[:, b, 0:256], a[rows, t, j, :], p[rows, :],
                                            start=m == 0, stop=m == 2)
                    return last
                nonlocal v_read
                done = soft["pv"] = v_read = PE.do([*state["pt"], *v_marks[t], free["pv"]], run, s_pv)

                def evacuated(marks):
                    ot_marks[t] = marks
                    free["pv"] = marks[1]
                split_later(base, AT["v_hi"], AT["v_lo"],
                            pv_bank[:, :, 0:256].rearrange("p b (h n) -> p b h n", h=GROUP),
                            ot_hi[:, t, :, :, :].rearrange("p h b n -> p b h n"),
                            ot_lo[:, t, :, :, :].rearrange("p h b n -> p b h n"),
                            [done, ot_free[t]], s_othi, s_otlo, evacuated)

            for when, work in (("tq", transpose_q), ("s", scores), ("s_add", bias_and_peak), ("s_exp", exponential),
                               ("s_norm", normalise), ("tp", transpose_p), ("v", values)):
                at(base, AT[when], work)

        soft = {"score": None, "prob": ones_done, "pv": bias_read[0]}
        kt_read = v_read = setup_read

        def width_step(unit, t, b, last_tile, waits, tail=None):
            cols = slice(t * P, (t + 1) * P)
            for c in range(QUARTERS):
                terms = [(act_hi[:, kt, cols], act_lo[:, kt, cols], *unit.wide(kt)) for kt in (2 * c, 2 * c + 1)]
                extra = []
                if c == QUARTERS - 1 and tail is not None:
                    tail_terms, extra = tail()
                    terms += tail_terms
                done = PE.do([main_free[b], *act_marks[t], *unit.marks[c], *waits, *extra],
                             lambda e, c=c, terms=terms: products(e, main_bank[b][:, :], terms, c == 0,
                                                                  c == QUARTERS - 1), s_main)
                if last_tile:
                    slot_free[unit.slot][c] = done
                if c < QUARTERS - 1:
                    tick()
            return done

        def kv_step(blk, pair, t, unit):
            b = next_bank()
            done = width_step(unit, t, b, t == TILES - 1, [])
            tick()
            base = quarter[0]
            bank = main_bank[b]
            cols_v = bank[:, 2 * HD:4 * HD].rearrange("p (j n) -> p j n", j=2)
            v_done_hi = AC.do([done, v_read], lambda e: e.activation(v_hi[:, t, :, :], cols_v, ACT.Copy), s_vhi)

            def low_half_of_v(squared):
                v_marks[t] = [v_done_hi, VE.do([v_done_hi, squared, v_read], lambda e: e.tensor_tensor(
                    v_lo[:, t, :, :], cols_v, f32(v_hi[:, t, :, :]), ALU.subtract), s_vlo)]

            def gain_and_transpose(dst, scaled, slot):
                gain = kgain[:, :].rearrange("p (o n) -> p o n", o=1).broadcast_to([P, 2, HD])
                d3 = dst[:, 0:2 * HD].rearrange("p (j n) -> p j n", j=2)
                gained = VE.do([scaled, gains], lambda e: e.tensor_tensor(d3, d3, gain, ALU.mult), s_qn)
                at(base, AT["tq"], lambda: key_transpose(base, dst, gained, slot, t))
            rms_norm(bank, b, 2, done, low_half_of_v, gain_and_transpose)

        def q_step(blk, g, t, unit):
            b = next_bank()
            done = width_step(unit, t, b, t == TILES - 1, [])
            act_free[t] = done
            tick()
            base = quarter[0]
            rms_norm(main_bank[b], b, GROUP, done, lambda squared: None,
                     lambda dst, scaled, slot: attend(base, g, t, dst, scaled, slot))

        def o_step(blk, g, t, unit):
            for half_no in range(2):
                b = next_bank()
                oc = slice(half_no * WIDE, (half_no + 1) * WIDE)
                for c in range(2):
                    terms = [(ot_hi[:, t, h, :, :].rearrange("p b n -> p (b n)"),
                              ot_lo[:, t, h, :, :].rearrange("p b n -> p (b n)"),
                              unit.hi(h)[:, oc], unit.lo(h)[:, oc]) for h in (2 * c, 2 * c + 1)]
                    marks = [m for h in (2 * c, 2 * c + 1) for m in unit.marks[h]]
                    done = PE.do([main_free[b], *ot_marks[t], *marks],
                                 lambda e, b=b, c=c, terms=terms: products(e, main_bank[b][:, :], terms, c == 0,
                                                                           c == 1), s_main)
                    if half_no == 1 and t == TILES - 1:
                        for h in (2 * c, 2 * c + 1):
                            slot_free[unit.slot][h] = done
                    tick()

                def accumulate(b=b, oc=oc, done=done):
                    main_free[b] = VE.do([done, x_here[t]], lambda e: e.tensor_tensor(
                        acc[:, t, oc], main_bank[b][:, :], acc[:, t, oc], ALU.add), s_acc)
                    acc_mark[t] = main_free[b]
                later(AT["add"], accumulate)
            ot_free[t] = done
            if g == KV_HEADS - 1:
                later(AT["x1"], lambda: transpose_x1(t))
                if t % 2 == 1:
                    later(AT["low"], lambda: low_rank(blk, t // 2))

        acc_mark = [None] * TILES
        low_marks = [None] * TILES

        def transpose_x1(t):
            for half_no, (name, bank) in enumerate((("qt", qt_bank), ("s", s_bank))):
                def run(e, half_no=half_no, bank=bank):
                    for k in range(4):
                        kt = 4 * half_no + k
                        last = e.transpose(bank[:, k * P:(k + 1) * P], acc[:, t, kt * P:(kt + 1) * P], ident[:, :])
                    return last
                done = PE.do([acc_mark[t], free[name], const], run, s_tr)
                evacuate_act(t, half_no, name, bank, done)
            acc_mark[t] = PO.do([done, bias_done], lambda e: e.tensor_tensor(
                acc[:, t, :], acc[:, t, :], bias_eff[:, :], ALU.add), s_bias2)

        s_bias2 = sig("s_bias2")
        low_h = qt_hi[:, :, :, :].rearrange("p b h n -> p (b h n)")
        low_l = qt_lo[:, :, :, :].rearrange("p b h n -> p (b h n)")

        def low_rank(blk, pair):
            n_batch = 2 * BPT
            cols = slice(2 * pair * P, (2 * pair + 2) * P)

            def run(e):
                terms = [(loraa_hi[:, kt, :], loraa_lo[:, kt, :], act_hi[:, kt, cols], act_lo[:, kt, cols])
                         for kt in range(KT)]
                return products(e, pt_bank[:, 0:2 * P], terms, True, True)
            done = PE.do([*act_marks[2 * pair], *act_marks[2 * pair + 1], *loraa_marks, free["pt"]], run, s_low)
            first = blk * TILES * BPT + pair * n_batch
            chosen = admask[:, first:first + n_batch].rearrange("p (b o) -> p b o", o=1)\
                .broadcast_to([P, n_batch, SEQ])
            masked = VE.do([done, soft["prob"], soft["low"]], lambda e: e.tensor_tensor(
                prob[:, :].rearrange("p (b n) -> p b n", b=n_batch),
                pt_bank[:, 0:2 * P].rearrange("p (b n) -> p b n", b=n_batch), chosen, ALU.mult), s_lowm)
            free["pt"] = masked
            marks = split(prob[:, :], low_h[:, cols], low_l[:, cols], [masked, qt_free[0]], [], s_lowhi, s_lowlo)
            low_marks[2 * pair] = low_marks[2 * pair + 1] = marks
            soft["low"] = marks[1]

        soft["low"] = None

        def f_step(blk, u, t, unit):
            b = next_bank()
            cols = slice(t * P, (t + 1) * P)
            oc = slice(u * WIDE, (u + 1) * WIDE)

            def tail():
                return [(low_h[:, cols], low_l[:, cols], beff_hi[:, oc], beff_lo[:, oc])], \
                    [*low_marks[t], *beff_marks]
            done = width_step(unit, t, b, t == TILES - 1, [], tail)
            tick()
            if u == 1:
                act_free[t] = done
                qt_free[0] = done

            def finish():
                main_free[b] = VE.do([done, acc_mark[t]], lambda e: e.tensor_tensor(
                    acc[:, t, oc], main_bank[b][:, :], acc[:, t, oc], ALU.add), s_acc)
                if u == 1:
                    stored = PO.do([main_free[b]], lambda e: e.dma_start(out[blk * TILES + t], acc[:, t, :]),
                                   s_out[t], 16)
                    acc_free[t] = [stored]

            def reload():
                x_here[t] = load_x(blk + 1, t)
            later(AT["add"], finish)
            if u == 1 and blk + 1 < BLOCKS:
                later(AT["reload"], reload)
                later(AT["mix_split"], lambda: mix_split(t))
                later(AT["mix"], lambda: mix_products(t))

        def prepare_ahead():
            later(AT["w_lo"] - AT["w_hi"], prepare_next())

        for u, (kind, blk, n) in enumerate(schedule):
            if kind == "kv":
                kt_free = kt_read
                v_free = v_read
            step = {"kv": kv_step, "q": q_step, "o": o_step, "f": f_step}[kind]
            for t in range(TILES):
                if u > 0:
                    later(AT["w_hi"], prepare_ahead)
                if (kind, blk, n, t) == ("kv", 0, 0, 0):
                    mix_split(3)
                if (kind, blk, n) == ("kv", 0, 0) and t in (1, 2):
                    mix_products(t + 1)
                step(blk, n, t, units[u])
        while side:
            tick()
        PO.do([*f_done, *(m for marks in acc_free for m in marks)], lambda e: e.memset(half[:, :], -0.5), s_mset)

        block = ctx.enter_context(nc.Block())

        @block.sync
        def _(eng):
            SP.emit(eng)

        @block.gpsimd
        def _(eng):
            PO.emit(eng)

        @block.scalar
        def _(eng):
            AC.emit(eng)

        @block.vector
        def _(eng):
            VE.emit(eng)

        @block.tensor
        def _(eng):
            PE.emit(eng)


def _wide_units(w, n_units):
    return w.reshape(UNIT_CHUNKS, 2, P, n_units, WIDE).transpose(3, 0, 2, 1, 4).reshape(
        n_units, UNIT_CHUNKS, P, CHUNK)


def _by_parity():
    frequency = (np.arange(DM) + 1) // 2
    return np.concatenate([np.flatnonzero(frequency % 2 == 0), np.flatnonzero(frequency % 2 == 1)])


def _basis():
    n = DM
    at = np.arange(n // 2)
    rows = np.zeros((n, n // 2))
    rows[0] = math.sqrt(n) / n
    f = np.arange(1, (n - 1) // 2 + 1)
    angle = 2 * math.pi * ((f[:, None] * at[None, :]) % n) / n
    rows[1:n - 1:2] = math.sqrt(n / 2.0) * 2 / n * np.cos(angle)
    rows[2:n:2] = math.sqrt(n / 2.0) * 2 / n * np.sin(angle)
    rows[n - 1] = math.sqrt(n) / n * np.where(at % 2 == 0, 1.0, -1.0)
    return rows.astype(np.float32)


def _alibi():
    start = 2 ** (-2 ** (-(math.log2(HEADS) - 3)))
    slopes = np.array([start * start ** i for i in range(HEADS)], dtype=np.float32)
    pos = np.arange(SEQ, dtype=np.float32)
    rel = pos[None, :] - pos[:, None]
    table = np.where(rel > 0, np.float32(-1e30), slopes[:, None, None] * rel).astype(np.float32)
    return table.reshape(HEADS // 2, 2, SEQ, SEQ).transpose(1, 2, 0, 3).reshape(P, HEADS // 2, SEQ)


def kernel(x, itok_B_0_15, itok_B_1_7, L0_cond_weights, L0_attn_Wq, L0_attn_Wk, L0_attn_Wv, L0_attn_Wo,
           L0_attn_q_norm_w, L0_attn_k_norm_w, L0_cond2_weight, L0_cond2_bias, L0_cond2_lora_a_weights,
           L0_cond2_lora_b_weights, L0_cond2_scaling_factors, L0_ffn_W_base, L0_ffn_b_base, L0_ffn_enc0,
           L0_ffn_enc1, L0_ffn_coefs0, L0_ffn_coefs1, L0_ffn_mask0, L0_ffn_mask1):
    import concourse.bacc as bacc
    from concourse.bass_utils import run_bass_kernel_spmd

    A = np.asarray
    wk = A(L0_attn_Wk).reshape(4, 2 * HD, DM)
    wv = A(L0_attn_Wv).reshape(4, 2 * HD, DM)
    wkv = np.concatenate([wk, wv], axis=1).reshape(4 * WIDE, DM)
    coefs = np.concatenate([A(L0_ffn_coefs0), A(L0_ffn_coefs1)], axis=2)
    masks = np.concatenate([A(L0_ffn_mask0), A(L0_ffn_mask1)], axis=2)

    def by_row(a):
        return a[:, _by_parity()].reshape(EXPERTS, KT, P, ENC).transpose(2, 0, 1, 3).reshape(P, EXPERTS * KT * ENC)

    w2 = A(L0_cond2_weight).reshape(KT, P, KT, P).transpose(2, 1, 0, 3).reshape(KT, P, CHUNK)
    lora_b = A(L0_cond2_lora_b_weights).transpose(1, 0, 2).reshape(KT, P, P).transpose(1, 0, 2).reshape(1, P, CHUNK)
    host = {
        "x": A(x).reshape(TOKENS // P, P, DM),
        "mix_of_batch": A(itok_B_0_15).reshape(1, BATCH),
        "adapter_of_batch": np.broadcast_to(A(itok_B_1_7).reshape(1, BATCH), (P, BATCH)),
        "adapter_of_row": (np.arange(P) // RANK).astype(np.float32).reshape(P, 1),
        "adapter_scale": np.repeat(A(L0_cond2_scaling_factors), RANK).reshape(P, 1),
        "mix_w": A(L0_cond_weights),
        "wq": _wide_units(A(L0_attn_Wq).T, KV_HEADS),
        "wkv": _wide_units(wkv.T, 4),
        "wo": A(L0_attn_Wo).T.reshape(KV_HEADS, GROUP, HD, DM),
        "q_norm_w": np.broadcast_to(A(L0_attn_q_norm_w), (P, HD)),
        "k_norm_w": np.broadcast_to(A(L0_attn_k_norm_w), (P, HD)),
        "w2_units": np.concatenate([w2, lora_b], axis=0),
        "b2": A(L0_cond2_bias).reshape(KT, P).T,
        "lora_a": A(L0_cond2_lora_a_weights).reshape(P, KT, P).transpose(2, 1, 0).reshape(P, CHUNK),
        "w_base": _wide_units(A(L0_ffn_W_base).T, 2),
        "b_base": np.broadcast_to(A(L0_ffn_b_base), (P, DM)),
        "encoders": np.concatenate([A(L0_ffn_enc0), A(L0_ffn_enc1)], axis=0),
        "coefs": by_row(coefs),
        "masks": by_row(masks),
        "basis": _wide_units(_basis()[_by_parity()], 1),
        "alibi": _alibi(),
        "identity": np.eye(P, dtype=np.float32),
    }
    nc = bacc.Bacc("TRN2", target_bir_lowering=False, num_devices=1)
    arrays, aps = {}, {}
    for name, a in host.items():
        a = np.ascontiguousarray(a)
        arrays[f"in_{name}"] = a
        aps[name] = nc.dram_tensor(f"in_{name}", a.shape, mybir.dt.from_np(a.dtype), kind="ExternalInput").ap()
    out = nc.dram_tensor("out_tokens", (TOKENS // P, P, DM), F32, kind="ExternalOutput").ap()
    build_program(nc, aps, out)
    r = run_bass_kernel_spmd(nc, [arrays], core_ids=[0])
    return r.results[0]["out_tokens"].reshape(BATCH, SEQ, DM)
```
